# Optimizing a Trainium2 kernel written in Bass

```python
import numpy as np
import jax
import jax.numpy as jnp

def _softmax(x, axis=-1):
    return jax.nn.softmax(x, axis=axis)

def _gelu(x):
    return jax.nn.gelu(x, approximate=True)

def _silu(x):
    return jax.nn.silu(x)

def _sigmoid(x):
    return jax.nn.sigmoid(x)

def _layernorm(x, axis=-1, eps=1e-05):
    m = jnp.mean(x, axis=axis, keepdims=True)
    v = jnp.var(x, axis=axis, keepdims=True)
    return (x - m) / jnp.sqrt(v + eps)

def _scatter_add(tgt, idx, src, axis=0):
    return tgt.at[idx].add(src)

def _segment_sum(src, seg, n):
    return jax.ops.segment_sum(src, seg, n)
kernel_name = 'mk_lm_tower_d1_tok_ids2048_r4_bf4629'

def setup_inputs(seed: int=0):
    np.random.seed(seed)
    _w = jnp.asarray

    def _rec_inputs():
        import jax
        import jax.numpy as jnp
        _rk = jax.random.key(seed)
        x = jax.random.randint(jax.random.fold_in(_rk, 1), (16, 128), 0, 127998, jnp.int32)
        return x
    x = _rec_inputs()

    def _L0_tok_setup():
        import jax, jax.numpy as jnp
        import numpy as np
        VOCAB, D_EMBED, D_MODEL = (32000, 128, 512)
        key = jax.random.key(seed)
        k_ids, k_e, k_p = jax.random.split(key, 3)
        token_ids = jax.random.randint(k_ids, (4, 1024), 0, VOCAB)
        E = jax.random.normal(k_e, (VOCAB, D_EMBED), dtype=jnp.float32)
        bound = 1.0 / np.sqrt(D_EMBED)
        P = jax.random.uniform(k_p, (D_MODEL, D_EMBED), dtype=jnp.float32, minval=-bound, maxval=bound)
        return {'token_ids': token_ids, 'E': E, 'P': P}
    _L0_tok_all = _L0_tok_setup()
    _L0_tok_in = {k: v for k, v in _L0_tok_all.items() if k in ('E', 'P')}
    del _L0_tok_all

    def _L0_attn_setup():
        import jax, jax.numpy as jnp
        import numpy as np
        NUM_HEADS = 16
        CHUNK = 64
        RMS_EPS = 1.1920928955078125e-07

        def _forward(x, w_in, w_out):
            B, S, D = x.shape
            H, hd, C = (NUM_HEADS, D // NUM_HEADS, CHUNK)
            proj = x @ w_in.T
            q, k, v, a, g = jnp.split(proj, 5, axis=-1)
            rs = lambda t: t.reshape(B, S, H, hd)
            q, k, v, a, g = map(rs, (q, k, v, a, g))
            q = q * jax.lax.rsqrt(jnp.mean(q * q, axis=-1, keepdims=True) + RMS_EPS)
            k = jnp.tanh(k)
            a = jnp.clip(jax.nn.sigmoid(a + 2.0), 0.6, 0.9995)
            u = k * v
            NC = S // C
            a_r = a.reshape(B, NC, C, H, hd).transpose(1, 0, 2, 3, 4)
            u_r = u.reshape(B, NC, C, H, hd).transpose(1, 0, 2, 3, 4)

            def step(state, au):
                a_c, u_c = au
                prefix = jnp.cumprod(a_c, axis=1)
                acc = jnp.cumsum(u_c / jnp.maximum(prefix, 1e-06), axis=1)
                states = prefix * (state[:, None] + acc)
                return (states[:, -1], states)
            state0 = jnp.zeros((B, H, hd), dtype=jnp.float32)
            _, mem = jax.lax.scan(step, state0, (a_r, u_r))
            memory = mem.transpose(1, 0, 2, 3, 4).reshape(B, S, H, hd)
            gate = jax.nn.sigmoid(g)
            y = gate * (q * memory) + (1.0 - gate) * v
            return y.reshape(B, S, D) @ w_out.T
        key = jax.random.key(seed)
        k1, k2, k3 = jax.random.split(key, 3)
        B, S, D = (2, 1024, 512)
        x = jax.random.normal(k1, (B, S, D), dtype=jnp.float32)
        w_in = jax.random.normal(k2, (5 * D, D), dtype=jnp.float32) * 0.02
        w_out = jax.random.normal(k3, (D, D), dtype=jnp.float32) * 0.02
        return {'x': x, 'w_in': w_in, 'w_out': w_out}
    _L0_attn_all = _L0_attn_setup()
    _L0_attn_in = {k: v for k, v in _L0_attn_all.items() if k in ('w_in', 'w_out')}
    del _L0_attn_all

    def _L0_ffn_setup():
        import jax, jax.numpy as jnp
        import numpy as np
        BLOCK_SIZE = 32
        HIDDEN_SIZE = 512
        MLP_DIM = 4096
        NVFP4_LUT = jnp.array([0.0, 0.5, 1.0, 1.5, 2.0, 3.0, 4.0, 6.0, 0.0, -0.5, -1.0, -1.5, -2.0, -3.0, -4.0, -6.0], dtype=jnp.float32)

        def dequant_nvfp4(W_packed, scales, block=BLOCK_SIZE):
            N = W_packed.shape[0]
            low = W_packed & 15
            high = W_packed >> 4 & 15
            idx = jnp.stack([low, high], axis=-1).reshape(N, -1)
            vals = NVFP4_LUT[idx]
            K = vals.shape[1]
            vals = vals.reshape(N, K // block, block) * scales[:, :, None]
            return vals.reshape(N, K)
        key = jax.random.key(seed)
        ks = jax.random.split(key, 7)
        x = jax.random.normal(ks[0], (4, 32, HIDDEN_SIZE), dtype=jnp.float32)
        gate_W_packed = jax.random.randint(ks[1], (MLP_DIM, HIDDEN_SIZE // 2), 0, 64, dtype=jnp.int32)
        gate_scales = jax.random.uniform(ks[2], (MLP_DIM, HIDDEN_SIZE // BLOCK_SIZE), dtype=jnp.float32) * 0.1 + 0.001
        up_W_packed = jax.random.randint(ks[3], (MLP_DIM, HIDDEN_SIZE // 2), 0, 64, dtype=jnp.int32)
        up_scales = jax.random.uniform(ks[4], (MLP_DIM, HIDDEN_SIZE // BLOCK_SIZE), dtype=jnp.float32) * 0.1 + 0.001
        down_W_packed = jax.random.randint(ks[5], (HIDDEN_SIZE, MLP_DIM // 2), 0, 64, dtype=jnp.int32)
        down_scales = jax.random.uniform(ks[6], (HIDDEN_SIZE, MLP_DIM // BLOCK_SIZE), dtype=jnp.float32) * 0.1 + 0.001
        return {'x': x, 'gate_W_packed': gate_W_packed, 'gate_scales': gate_scales, 'up_W_packed': up_W_packed, 'up_scales': up_scales, 'down_W_packed': down_W_packed, 'down_scales': down_scales}
    _L0_ffn_all = _L0_ffn_setup()
    _L0_ffn_in = {k: v for k, v in _L0_ffn_all.items() if k in ('gate_W_packed', 'gate_scales', 'up_W_packed', 'up_scales', 'down_W_packed', 'down_scales')}
    del _L0_ffn_all
    return {'x': x, 'L0_tok_E': _L0_tok_in['E'], 'L0_tok_P': _L0_tok_in['P'], 'L0_attn_w_in': _L0_attn_in['w_in'], 'L0_attn_w_out': _L0_attn_in['w_out'], 'L0_ffn_gate_W_packed': _L0_ffn_in['gate_W_packed'], 'L0_ffn_gate_scales': _L0_ffn_in['gate_scales'], 'L0_ffn_up_W_packed': _L0_ffn_in['up_W_packed'], 'L0_ffn_up_scales': _L0_ffn_in['up_scales'], 'L0_ffn_down_W_packed': _L0_ffn_in['down_W_packed'], 'L0_ffn_down_scales': _L0_ffn_in['down_scales']}

def reference(x, L0_tok_E, L0_tok_P, L0_attn_w_in, L0_attn_w_out, L0_ffn_gate_W_packed, L0_ffn_gate_scales, L0_ffn_up_W_packed, L0_ffn_up_scales, L0_ffn_down_W_packed, L0_ffn_down_scales):
    import jax
    import jax.numpy as jnp

    def _L0_tok_ref(token_ids, E, P):
        import jax, jax.numpy as jnp
        import numpy as np
        VOCAB, D_EMBED, D_MODEL = (32000, 128, 512)
        emb = E[token_ids]
        return jnp.einsum('bse,me->bsm', emb, P)

    def _L0_attn_ref(x, w_in, w_out):
        import jax, jax.numpy as jnp
        import numpy as np
        NUM_HEADS = 16
        CHUNK = 64
        RMS_EPS = 1.1920928955078125e-07

        def _forward(x, w_in, w_out):
            B, S, D = x.shape
            H, hd, C = (NUM_HEADS, D // NUM_HEADS, CHUNK)
            proj = x @ w_in.T
            q, k, v, a, g = jnp.split(proj, 5, axis=-1)
            rs = lambda t: t.reshape(B, S, H, hd)
            q, k, v, a, g = map(rs, (q, k, v, a, g))
            q = q * jax.lax.rsqrt(jnp.mean(q * q, axis=-1, keepdims=True) + RMS_EPS)
            k = jnp.tanh(k)
            a = jnp.clip(jax.nn.sigmoid(a + 2.0), 0.6, 0.9995)
            u = k * v
            NC = S // C
            a_r = a.reshape(B, NC, C, H, hd).transpose(1, 0, 2, 3, 4)
            u_r = u.reshape(B, NC, C, H, hd).transpose(1, 0, 2, 3, 4)

            def step(state, au):
                a_c, u_c = au
                prefix = jnp.cumprod(a_c, axis=1)
                acc = jnp.cumsum(u_c / jnp.maximum(prefix, 1e-06), axis=1)
                states = prefix * (state[:, None] + acc)
                return (states[:, -1], states)
            state0 = jnp.zeros((B, H, hd), dtype=jnp.float32)
            _, mem = jax.lax.scan(step, state0, (a_r, u_r))
            memory = mem.transpose(1, 0, 2, 3, 4).reshape(B, S, H, hd)
            gate = jax.nn.sigmoid(g)
            y = gate * (q * memory) + (1.0 - gate) * v
            return y.reshape(B, S, D) @ w_out.T
        return _forward(x, w_in, w_out)

    def _L0_ffn_ref(x, gate_W_packed, gate_scales, up_W_packed, up_scales, down_W_packed, down_scales):
        import jax, jax.numpy as jnp
        import numpy as np
        BLOCK_SIZE = 32
        HIDDEN_SIZE = 512
        MLP_DIM = 4096
        NVFP4_LUT = jnp.array([0.0, 0.5, 1.0, 1.5, 2.0, 3.0, 4.0, 6.0, 0.0, -0.5, -1.0, -1.5, -2.0, -3.0, -4.0, -6.0], dtype=jnp.float32)

        def dequant_nvfp4(W_packed, scales, block=BLOCK_SIZE):
            N = W_packed.shape[0]
            low = W_packed & 15
            high = W_packed >> 4 & 15
            idx = jnp.stack([low, high], axis=-1).reshape(N, -1)
            vals = NVFP4_LUT[idx]
            K = vals.shape[1]
            vals = vals.reshape(N, K // block, block) * scales[:, :, None]
            return vals.reshape(N, K)
        B, S, H = x.shape
        xt = x.reshape(B * S, H)
        Wg = dequant_nvfp4(gate_W_packed, gate_scales)
        Wu = dequant_nvfp4(up_W_packed, up_scales)
        Wd = dequant_nvfp4(down_W_packed, down_scales)
        gate = jnp.einsum('th,nh->tn', xt, Wg)
        up = jnp.einsum('th,nh->tn', xt, Wu)
        gelu = jnp.tanh(0.7978845608028654 * (gate + 0.044715 * gate ** 3)) * gate * 0.5 + gate * 0.5
        inter = gelu * up
        out = jnp.einsum('tn,hn->th', inter, Wd)
        return out.reshape(B, S, H)
    h = _L0_tok_ref(x, L0_tok_E, L0_tok_P)
    h = h + _L0_attn_ref(_layernorm(h, axis=-1), L0_attn_w_in, L0_attn_w_out)
    h = h + _L0_ffn_ref(_layernorm(h, axis=-1), L0_ffn_gate_W_packed, L0_ffn_gate_scales, L0_ffn_up_W_packed, L0_ffn_up_scales, L0_ffn_down_W_packed, L0_ffn_down_scales)
    return h

_drawn_inputs = setup_inputs


def setup_inputs(seed=0):
    import zlib

    import numpy as np

    out = dict(_drawn_inputs(seed))
    spreads = {}
    factors = {}
    for name, (base, spread) in spreads.items():
        noise = np.random.default_rng([zlib.crc32(name.encode()), seed]).standard_normal(out[name].shape)
        drawn = base * np.exp(spread * noise) if base else spread * noise
        out[name] = jnp.asarray(drawn.astype(out[name].dtype))
    for name, factor in factors.items():
        out[name] = (out[name] * factor).astype(out[name].dtype)
    return out
```

```python
from contextlib import ExitStack

import concourse.bass as bass
from concourse import mybir

F32 = mybir.dt.float32
F16 = mybir.dt.float16
I32 = mybir.dt.int32
U32 = mybir.dt.uint32
ALU = mybir.AluOpType
ACT = mybir.ActivationFunctionType
AX_X = mybir.AxisListType.X

P = 128
SEQS, SEQ_LEN = 16, 128
VOCAB, D_EMBED, D = 32000, 128, 512
MLP = 4096
HEADS, HEAD_DIM, CHUNK = 16, 32, 64
TOKENS = SEQS * SEQ_LEN
TILE = 512
TILES = TOKENS // TILE
BLOCKS = TILE // P
KT = D // P
CT = D // P
SECTIONS = 5
RMS_EPS, LN_EPS = 1.1920928955078125e-07, 1e-05
A_LO, A_HI, PREFIX_LO = 0.6, 0.9995, 1e-06
BLK = 32
GROUP = 4
GROUPS = MLP // (GROUP * P)
PAIRS = GROUPS // 2
STEPS = TILES * GROUP
WORDS = 1024

W_EXP = 14
F_EXP = 12
CODE_EXP = 14
X_EXP = 11
Y_EXP = -5
I_EXP = -11
GELU_A, GELU_C = 0.044715, 0.7978845608028654

JOBS = 7
MAXES = 9


class Steps:

    def __init__(self, eng, sem):
        self.eng, self.sem, self.n = eng, sem, 0

    def mark(self, instruction):
        instruction.then_inc(self.sem, 1)
        self.n += 1

    def settle(self):
        self.eng.wait_ge(self.sem, self.n)

    def run(self, instruction):
        self.mark(instruction)
        self.settle()

    def restart(self):
        self.settle()
        self.eng.sem_clear(self.sem)
        self.n = 0


def lm_layer(nc, ids, table, p_t, w_in, w_out, all_scales, packed, scales, out):
    with ExitStack() as ctx:
        def sb(name, shape, dt):
            return ctx.enter_context(nc.sbuf_tensor(name, shape, dt))

        def sem(name):
            return ctx.enter_context(nc.semaphore(name))

        h = sb("h", [P, SEQS, D], F32)
        xT = sb("xT", [P, 2, KT, TOKENS], F16)
        region = sb("region", [P, 10240], F32)
        win = region[:, :].bitcast(F16).rearrange("p (s k m) -> p s k m", s=2, k=KT)
        wout = sb("wout", [P, 2, CT, D], F16)
        even_w = sb("even_w", [P, 2, 3, GROUP, D], F16)
        odd_w = region[:, 0:6144].bitcast(F16).rearrange("p (s m n w) -> p s m n w", s=2, m=3, n=GROUP)
        ffn_w = [even_w, odd_w]
        sq = region[:, 6144:7168].rearrange("p (b t) -> p b t", b=2)
        th = region[:, 7168:8192].rearrange("p (b t) -> p b t", b=2)
        inter = region[:, 8192:9216].bitcast(F16).rearrange("p (b s t) -> p b s t", b=2, s=2)
        stage = sb("stage", [P, 2, 2048], F32)
        tk = sb("tk", [P, 2, TILE], F32)
        vs = sb("vs", [P, 2, TILE], F32)
        sa = sb("sa", [P, 2, TILE], F32)
        sg = sb("sg", [P, 2, TILE], F32)
        mem = sb("mem", [P, TILE], F32)
        starts = sb("starts", [P, TILE], F32)
        qs = sb("qs", [P, CT, TILE], F32)
        emb = qs[:, :, :].rearrange("p c (s e) -> p (c s) e", e=D_EMBED)
        q2 = sb("q2", [P, 2, TILE], F32)
        emb_t, pt_sb = q2[:, 0, :], q2[:, 1, :]
        yx = sb("yx", [P, 4 * TILE], F32)
        y_hl = yx[:, :].bitcast(F16).rearrange("p (s c t) -> p s c t", s=2, c=CT)
        xn = yx[:, :].rearrange("p (b d) -> p b d", b=BLOCKS)
        rinv = sb("rinv", [HEADS, TILE], F32)
        mag = sb("mag", [P, 512], I32)
        wf = sb("wf", [P, 2, 512], F32)
        ident = sb("ident", [P, P], F32)
        head_sum = sb("head_sum", [P, CT, HEADS], F32)
        head_spread = sb("head_spread", [HEADS, D], F32)
        bias = sb("bias", [P, 4], F32)
        ids_sb = sb("ids_sb", [P, SEQS], I32)
        ids_f = sb("ids_f", [P, 2, SEQS], F32)
        rows = sb("rows", [P, SEQS], I32)
        pmax = sb("pmax", [P, MAXES], F32)
        cmax = sb("cmax", [4, 1], F32)
        cmax_b = sb("cmax_b", [4, P], F32)
        p2 = sb("p2", [P, MAXES], F32)
        s_w = sb("s_w", [P, MAXES], F32)
        undo = sb("undo", [P, MAXES], F32)
        s_y = sb("s_y", [P, 1], F32)
        undo_out = sb("undo_out", [P, 1], F32)
        undo_down = sb("undo_down", [P, 1], F32)
        tanh_in = sb("tanh_in", [P, 1], F32)
        stats = sb("stats", [P, BLOCKS, 6], F32)
        mv = sb("mv", [P, BLOCKS, 2], F32)
        rstd = sb("rstd", [P, BLOCKS], F32)
        ps = ctx.enter_context(nc.psum_tensor("ps", [P, 8, TILE], F32))

        ids_in, pt_in, out_stored = sem("ids_in"), sem("pt_in"), sem("out_stored")
        emb_in = [sem(f"emb_in{t}") for t in range(TILES)]
        stage_in = [sem(f"stage_in{s}") for s in range(2)]
        raw_in = [sem(f"raw_in{s}") for s in range(2)]
        consts_ready, rows_ready, zeroed = sem("consts_ready"), sem("rows_ready"), sem("zeroed")
        pmax_ready, pmax_turned, cmax_ready, cmax_spread = (
            sem("pmax_ready"), sem("pmax_turned"), sem("cmax_ready"), sem("cmax_spread"))
        scale_ready, w_hi_done, w_done = sem("scale_ready"), sem("w_hi_done"), sem("w_done")
        emb_turned, emb_copied, h_made, h_copied = (
            sem("emb_turned"), sem("emb_copied"), sem("h_made"), sem("h_copied"))
        var_ready, std_ready, xn_ready, x_turned, x_hi_done, x_done = (
            sem("var_ready"), sem("std_ready"), sem("xn_ready"), sem("x_turned"), sem("x_hi_done"),
            sem("x_done"))
        q_made, q_copied, q_squared, sum_made, sum_rooted, rinv_ready, rinv_spread, q_normed = (
            sem("q_made"), sem("q_copied"), sem("q_squared"), sem("sum_made"), sem("sum_rooted"),
            sem("rinv_ready"), sem("rinv_spread"), sem("q_normed"))
        k_made, v_made, a_made, g_made = sem("k_made"), sem("v_made"), sem("a_made"), sem("g_made")
        k_tanh, v_copied, a_sig, g_sig = sem("k_tanh"), sem("v_copied"), sem("a_sig"), sem("g_sig")
        y_ready, y_hi_done, y_done = sem("y_ready"), sem("y_hi_done"), sem("y_done")
        attn_out, attn_added = sem("attn_out"), sem("attn_added")
        wf_ready, f_hi_done, f_done = sem("wf_ready"), sem("f_hi_done"), sem("f_done")
        gate_made, up_made, gate_squared, inner_ready, tanh_done, inter_ready, inter_hi, inter_done = (
            sem("gate_made"), sem("up_made"), sem("gate_squared"), sem("inner_ready"), sem("tanh_done"),
            sem("inter_ready"), sem("inter_hi"), sem("inter_done"))
        down_made, down_free = sem("down_made"), sem("down_free")
        dve_step, pool_step = sem("dve_step"), sem("pool_step")

        block = ctx.enter_context(nc.Block())

        def tile_cols(t):
            return bass.ts(t, TILE)

        def load_slot(n):
            return n % 2

        @block.sync
        def _(sp):
            sp.dma_start(ids_sb[:, :], ids).then_inc(ids_in, 16)
            sp.dma_start(pt_sb, p_t).then_inc(pt_in, 16)
            for j in range(JOBS):
                if j >= 2:
                    sp.wait_ge(w_done, j - 1)
                if j < SECTIONS:
                    src, dst = w_in[j], stage[:, j % 2, :]
                elif j == SECTIONS:
                    src, dst = w_out, stage[:, j % 2, :]
                else:
                    src, dst = all_scales, stage[:, j % 2, 0:1536]
                sp.dma_start(dst, src).then_inc(stage_in[j % 2], 16)

            def load_packed(n, slot):
                sp.dma_start(stage[:, slot, 0:WORDS].bitcast(I32), packed[n]).then_inc(raw_in[slot], 16)
                sp.dma_start(stage[:, slot, WORDS:], scales[n].unsqueeze(1).broadcast_to([8, 16, WORDS]))\
                  .then_inc(raw_in[slot], 16)

            sp.wait_ge(pmax_ready, JOBS)
            load_packed(0, 0)
            load_packed(1, 1)

            def later_loads(pair, count):
                for i in range(count):
                    n = 6 * pair + i + 2
                    sp.wait_ge(wf_ready, 4 * (6 * pair + i + 1))
                    load_packed(n, i % 2)

            with sp.Fori(0, PAIRS - 1) as pair:
                later_loads(pair, 6)
            later_loads(PAIRS - 1, 4)
            for t in range(TILES):
                sp.wait_ge(down_free, BLOCKS * ((GROUPS - 1) * TILES + t + 2))
                sp.dma_start(out[:, t * BLOCKS:(t + 1) * BLOCKS, :], h[:, t * BLOCKS:(t + 1) * BLOCKS, :])\
                  .then_inc(out_stored, 16)
            sp.wait_ge(out_stored, 16 * TILES)

        @block.gpsimd
        def _(pool):
            own = Steps(pool, pool_step)
            own.mark(nc.gpsimd.memset(ident[:, :], 0.0))
            own.mark(nc.gpsimd.memset(head_sum[:, :, :], 1.0))
            own.mark(nc.gpsimd.memset(head_spread[:, :], 1.0))
            own.settle()
            own.mark(nc.gpsimd.affine_select(out=ident[:, :], in_=ident[:, :], compare_op=ALU.not_equal,
                                             fill=1.0, base=0, pattern=[[-1, P]], channel_multiplier=1))
            hs = head_sum[:, :, :]
            own.run(nc.gpsimd.affine_select(out=hs, in_=hs, compare_op=ALU.is_ge, fill=0.0, base=0,
                                            pattern=[[P, CT], [-HEAD_DIM, HEADS]], channel_multiplier=1))
            own.run(nc.gpsimd.affine_select(out=hs, in_=hs, compare_op=ALU.is_ge, fill=0.0,
                                            base=HEAD_DIM - 1, pattern=[[-P, CT], [HEAD_DIM, HEADS]],
                                            channel_multiplier=-1))
            hp = head_spread[:, :]
            own.run(nc.gpsimd.affine_select(out=hp, in_=hp, compare_op=ALU.is_ge, fill=0.0, base=0,
                                            pattern=[[1, D]], channel_multiplier=-HEAD_DIM))
            own.run(nc.gpsimd.affine_select(out=hp, in_=hp, compare_op=ALU.is_ge, fill=0.0,
                                            base=HEAD_DIM - 1, pattern=[[-1, D]],
                                            channel_multiplier=HEAD_DIM))
            nc.gpsimd.memset(bias[:, 0:1], 2.0)
            nc.gpsimd.memset(bias[:, 1:2], RMS_EPS)
            nc.gpsimd.memset(bias[:, 2:3], LN_EPS).then_inc(consts_ready, 1)
            pool.wait_ge(rows_ready, 1)
            for s in range(SEQS):
                nc.gpsimd.indirect_dma_start(
                    out=emb[:, s, :], out_offset=None, in_=table,
                    in_offset=bass.IndirectOffsetOnAxis(ap=rows[:, s:s + 1].bitcast(U32), axis=0),
                ).then_inc(emb_in[s // BLOCKS], 16)

            def f_lo(n, par, m, half):
                for i in range(2):
                    k = 4 * n + 2 * half + i
                    pool.wait_ge(f_hi_done, k + 1)
                    nc.gpsimd.tensor_tensor(ffn_w[par][:, 1, m, 2 * half + i, :], wf[:, i, :],
                                            ffn_w[par][:, 0, m, 2 * half + i, :],
                                            ALU.subtract).then_inc(f_done, 1)

            def group_lo(n0, par):
                for m in range(3):
                    for half in range(2):
                        f_lo(n0 + m, par, m, half)

            group_lo(0, 0)
            group_lo(3, 1)
            with pool.Fori(1, PAIRS) as pair:
                group_lo(6 * pair, 0)
                group_lo(6 * pair + 3, 1)

        @block.scalar
        def _(act):
            def split_hi(j):
                act.wait_ge(scale_ready, j + 1)
                src = stage[:, j % 2, :]
                if j < SECTIONS:
                    dst = win[:, 0, :, j * D:(j + 1) * D]
                    src = src.rearrange("p (k m) -> p k m", k=KT)
                else:
                    dst = wout[:, 0, :, :].rearrange("p c m -> p (c m)")
                nc.scalar.activation(dst, src, ACT.Identity, scale=s_w[:, j:j + 1]).then_inc(w_hi_done, 1)

            def norm_tail(n, t):
                act.wait_ge(var_ready, n + 1)
                nc.scalar.activation(rstd[:, :], mv[:, :, 1], ACT.Sqrt, bias=bias[:, 2:3])\
                    .then_inc(std_ready, 1)
                for k in range(KT):
                    act.wait_ge(x_turned, KT * n + k + 1)
                    nc.scalar.activation(xT[:, 0, k, tile_cols(t)], ps[:, 4 + k, :], ACT.Copy)\
                        .then_inc(x_hi_done, 1)

            def prep(t):
                act.wait_ge(emb_turned, t + 1)
                nc.scalar.activation(emb_t, ps[:, 4, :], ACT.Copy).then_inc(emb_copied, 1)
                for b in range(BLOCKS):
                    act.wait_ge(h_made, BLOCKS * t + b + 1)
                    nc.scalar.activation(h[:, BLOCKS * t + b, :], ps[:, b % 3, :], ACT.Copy)\
                        .then_inc(h_copied, 1)
                norm_tail(t, t)

            def copy_q(t, c):
                act.wait_ge(q_made, CT * t + c + 1)
                nc.scalar.activation(qs[:, c, :], ps[:, 4 + c, :], ACT.Identity, scale=undo[:, 0:1])\
                    .then_inc(q_copied, 1)

            def square_q(t, c, waits=True):
                act.wait_ge(q_copied, CT * t + c + 1)
                if c >= 2:
                    act.wait_ge(sum_made, CT * t + c - 1)
                nc.scalar.activation(q2[:, c % 2, :], qs[:, c, :], ACT.Square).then_inc(q_squared, 1)

            def root_sums(t):
                act.wait_ge(sum_made, CT * t + CT)
                nc.scalar.activation(rinv[:, :], ps[0:HEADS, 3, :], ACT.Sqrt, bias=bias[0:HEADS, 1:2],
                                     scale=1.0 / HEAD_DIM).then_inc(sum_rooted, 1)

            def unit(t, c, first=False):
                u, b = CT * t + c, c % 2
                if not (first and c < 2):
                    act.wait_ge(y_ready, u - 1)
                act.wait_ge(k_made, u + 1)
                nc.scalar.activation(tk[:, b, :], ps[:, 0, :], ACT.Tanh, scale=undo[:, 1:2])\
                    .then_inc(k_tanh, 1)
                act.wait_ge(v_made, u + 1)
                nc.scalar.activation(vs[:, b, :], ps[:, 1, :], ACT.Identity, scale=undo[:, 2:3])\
                    .then_inc(v_copied, 1)
                act.wait_ge(a_made, u + 1)
                nc.scalar.activation(sa[:, b, :], ps[:, 2, :], ACT.Sigmoid, bias=bias[:, 0:1],
                                     scale=undo[:, 3:4]).then_inc(a_sig, 1)
                if not (first and c < 2):
                    act.wait_ge(y_done, u - 1)
                act.wait_ge(g_made, u + 1)
                nc.scalar.activation(sg[:, b, :], ps[:, 3, :], ACT.Sigmoid, scale=undo[:, 4:5])\
                    .then_inc(g_sig, 1)

            def y_hi(t, c):
                act.wait_ge(y_ready, CT * t + c + 1)
                nc.scalar.activation(y_hl[:, 0, c, :], sg[:, c % 2, :], ACT.Identity, scale=s_y[:, 0:1])\
                    .then_inc(y_hi_done, 1)

            def f_hi(n, par, m, half):
                for i in range(2):
                    act.wait_ge(wf_ready, 4 * n + 2 * half + i + 1)
                    nc.scalar.activation(ffn_w[par][:, 0, m, 2 * half + i, :], wf[:, i, :], ACT.Copy)\
                        .then_inc(f_hi_done, 1)

            def attention(t, first=False, last=False):
                for c in range(CT):
                    unit(t, c, first)
                    if c > 0:
                        y_hi(t, c - 1)
                    if last and c > 0:
                        f_hi(c - 1, 0, c - 1, 0)
                        f_hi(c - 1, 0, c - 1, 1)
                y_hi(t, CT - 1)
                if not last:
                    for c in range(2):
                        copy_q(t + 1, c)
                    for c in range(2):
                        square_q(t + 1, c)
                    for c in range(2, CT):
                        copy_q(t + 1, c)
                    for c in range(2, CT):
                        square_q(t + 1, c)
                norm_tail(TILES + t, t)
                if not last:
                    root_sums(t + 1)

            def ffn_step(s, index):
                b = s % 2
                act.wait_ge(gate_made, index + 1)
                nc.scalar.activation(sq[:, b, :], ps[:, 4 + 2 * b, :], ACT.Square, scale=undo[:, 6:7])\
                    .then_inc(gate_squared, 1)
                act.wait_ge(inner_ready, index + 1)
                nc.scalar.activation(th[:, b, :], sq[:, b, :], ACT.Tanh, scale=tanh_in[:, 0:1])\
                    .then_inc(tanh_done, 1)

            def inter_high(s, index):
                act.wait_ge(inter_ready, index + 1)
                nc.scalar.activation(inter[:, s % 2, 0, :], th[:, s % 2, :], ACT.Copy).then_inc(inter_hi, 1)

            def ffn_group(group, par, last=False):
                for s in range(STEPS):
                    index = STEPS * group + s
                    ffn_step(s, index)
                    if s >= 2 and s % 2 == 0 and s <= 12 and not last:
                        piece = (s - 2) // 2
                        f_hi(3 * (group + 1) + piece // 2, 1 - par, piece // 2, piece % 2)
                    inter_high(s, index)

            act.wait_ge(consts_ready, 1)
            for t in range(TILES):
                split_hi(t)
                prep(t)
            split_hi(4)
            split_hi(5)
            act.wait_ge(scale_ready, JOBS)
            for c in range(CT):
                copy_q(0, c)
            for c in range(CT):
                square_q(0, c)
            root_sums(0)
            attention(0, first=True)
            with act.Fori(1, TILES - 1) as t:
                attention(t)
            attention(TILES - 1, last=True)
            with act.Fori(0, PAIRS - 1) as pair:
                ffn_group(2 * pair, 0)
                ffn_group(2 * pair + 1, 1)
            ffn_group(GROUPS - 2, 0)
            ffn_group(GROUPS - 1, 1, last=True)

        @block.tensor
        def _(pe):
            def products(dst, terms, sem_done=None, n=1):
                for i, (w, x) in enumerate(terms):
                    last = nc.tensor.matmul(dst, w, x, start=(i == 0), stop=(i == len(terms) - 1))
                if sem_done is not None:
                    last.then_inc(sem_done, n)

            def in_terms(sec, c, t):
                cols = slice(sec * D + c * P, sec * D + (c + 1) * P)
                return [(win[:, a, k, cols], xT[:, b, k, tile_cols(t)])
                        for k in range(KT) for a, b in ((0, 0), (0, 1), (1, 0))]

            def spread_max(j, cols):
                n = cols[1] - cols[0]
                pe.wait_ge(pmax_ready, j + 1)
                nc.tensor.transpose(ps[0:n, 3, 0:P], pmax[:, cols[0]:cols[1]], ident[:, :])\
                    .then_inc(pmax_turned, 1)
                pe.wait_ge(cmax_ready, j + 1)
                nc.tensor.matmul(ps[:, 3, 256:256 + n], cmax_b[0:n, :], ident[0:n, 0:n], start=True,
                                 stop=True).then_inc(cmax_spread, 1)

            def turn_tokens(n):
                pe.wait_ge(xn_ready, BLOCKS * n + BLOCKS)
                for k in range(KT):
                    nib, half = k // 2, k % 2
                    for b in range(BLOCKS):
                        src = xn[:, b, 256 * half:256 * half + 256].rearrange("p (m i) -> p i m", i=2)
                        last = nc.tensor.transpose(ps[:, 4 + k, b * P:(b + 1) * P], src[:, nib, :],
                                                   ident[:, :])
                    last.then_inc(x_turned, 1)

            def prep(t):
                pe.wait_ge(emb_in[t], 16 * BLOCKS)
                if t > 0:
                    pe.wait_ge(x_done, KT * t)
                for b in range(BLOCKS):
                    last = nc.tensor.transpose(ps[:, 4, b * P:(b + 1) * P], emb[:, BLOCKS * t + b, :],
                                               ident[:, :])
                last.then_inc(emb_turned, 1)
                pe.wait_ge(emb_copied, t + 1)
                if t == 0:
                    pe.wait_ge(pt_in, 16)
                for b in range(BLOCKS):
                    if BLOCKS * t + b >= 3:
                        pe.wait_ge(h_copied, BLOCKS * t + b - 2)
                    nc.tensor.matmul(ps[:, b % 3, :], emb_t[:, b * P:(b + 1) * P], pt_sb, start=True,
                                     stop=True).then_inc(h_made, 1)
                turn_tokens(t)

            def make_q(t, c):
                products(ps[:, 4 + c, :], in_terms(0, c, t), q_made)

            def sum_squares(t, c):
                pe.wait_ge(q_squared, CT * t + c + 1)
                nc.tensor.matmul(ps[0:HEADS, 3, :], head_sum[:, c, :], q2[:, c % 2, :], start=(c == 0),
                                 stop=(c == CT - 1)).then_inc(sum_made, 1)

            def spread_rinv(t):
                pe.wait_ge(rinv_ready, t + 1)
                for c in range(CT):
                    nc.tensor.matmul(ps[:, 4 + c, :], head_spread[:, c * P:(c + 1) * P], rinv[:, :],
                                     start=True, stop=True).then_inc(rinv_spread, 1)

            def unit(t, c, first=False):
                u = CT * t + c
                for i, (made, read) in enumerate(((k_made, k_tanh), (v_made, v_copied), (a_made, a_sig),
                                                  (g_made, g_sig))):
                    if not (first and c == 0):
                        pe.wait_ge(read, u)
                    if i == 3 and c == 0:
                        pe.wait_ge(sum_rooted, t + 1)
                    products(ps[:, i, :], in_terms(1 + i, c, t), made)

            def project(t, b, bank):
                products(ps[:, bank, :],
                         [(y_hl[:, x, c, b * P:(b + 1) * P], wout[:, w, c, :])
                          for c in range(CT) for x, w in ((0, 0), (0, 1), (1, 0))], attn_out)

            def attention(t, first=False, last=False):
                unit(t, 0, first)
                spread_rinv(t)
                for c in range(1, CT):
                    unit(t, c, first)
                if not last:
                    pe.wait_ge(q_normed, CT * t + CT)
                    make_q(t + 1, 0)
                    make_q(t + 1, 1)
                    pe.wait_ge(g_sig, CT * t + CT)
                pe.wait_ge(y_done, CT * t + CT)
                if last:
                    pe.wait_ge(q_normed, CT * t + CT)
                project(t, 0, 6)
                project(t, 1, 7)
                if not last:
                    pe.wait_ge(q_copied, CT * (t + 1) + 2)
                project(t, 2, 4)
                project(t, 3, 5)
                if not last:
                    sum_squares(t + 1, 0)
                    sum_squares(t + 1, 1)
                    pe.wait_ge(attn_added, BLOCKS * t + 2)
                    make_q(t + 1, 2)
                    make_q(t + 1, 3)
                    pe.wait_ge(q_copied, CT * (t + 1) + 4)
                turn_tokens(TILES + t)
                if not last:
                    sum_squares(t + 1, 2)
                    sum_squares(t + 1, 3)

            def gate_up(s, par, t):
                ni, b = s % GROUP, s % 2
                for m, made in ((0, gate_made), (1, up_made)):
                    products(ps[:, 4 + 2 * b + m, :],
                             [(ffn_w[par][:, w, m, ni, k * P:(k + 1) * P], xT[:, x, k, tile_cols(t)])
                              for k in range(KT) for w, x in ((0, 0), (0, 1), (1, 0))], made)

            def down(s, par, index, tile_index):
                ni = s % GROUP
                if ni == 0:
                    pe.wait_ge(down_free, BLOCKS * (tile_index + 1))
                pe.wait_ge(inter_done, index + 1)
                for b in range(BLOCKS):
                    for i, (x, w) in enumerate(((0, 0), (0, 1), (1, 0))):
                        last = nc.tensor.matmul(ps[:, b, :], inter[:, s % 2, x, b * P:(b + 1) * P],
                                                ffn_w[par][:, w, 2, ni, :],
                                                start=(ni == 0 and i == 0), stop=(ni == GROUP - 1 and i == 2))
                    if ni == GROUP - 1:
                        last.then_inc(down_made, 1)

            def ffn_group(group, par, last=False):
                for s in range(STEPS):
                    if s + 1 < STEPS:
                        gate_up(s + 1, par, (s + 1) // GROUP)
                    elif not last:
                        pe.wait_ge(f_done, 12 * (group + 2))
                        gate_up(0, 1 - par, 0)
                    down(s, par, STEPS * group + s, TILES * group + s // GROUP)

            pe.wait_ge(consts_ready, 1)
            for t in range(TILES):
                spread_max(t, (t, t + 1))
                prep(t)
            spread_max(4, (4, 5))
            spread_max(5, (5, 6))
            spread_max(6, (6, 9))
            pe.wait_ge(w_done, JOBS - 1)
            pe.wait_ge(x_done, KT * TILES)
            for c in range(CT):
                make_q(0, c)
            for c in range(CT):
                sum_squares(0, c)
            attention(0, first=True)
            with pe.Fori(1, TILES - 1) as t:
                attention(t)
            attention(TILES - 1, last=True)
            pe.wait_ge(f_done, 12)
            pe.wait_ge(x_done, 2 * KT * TILES)
            gate_up(0, 0, 0)
            with pe.Fori(0, PAIRS - 1) as pair:
                ffn_group(2 * pair, 0)
                ffn_group(2 * pair + 1, 1)
            ffn_group(GROUPS - 2, 0)
            ffn_group(GROUPS - 1, 1, last=True)

        @block.vector
        def _(dve):
            own = Steps(dve, dve_step)
            V = nc.vector

            def scale_of(j, cols):
                n = cols[1] - cols[0]
                dve.wait_ge(stage_in[j % 2], 16 * (j // 2 + 1))
                src = stage[:, j % 2, 0:n * 512].rearrange("p (n w) -> p n w", n=n) if n > 1 \
                    else stage[:, j % 2, :]
                V.tensor_reduce(pmax[:, cols[0]:cols[1]], src, AX_X, ALU.max, apply_absolute_value=True)\
                    .then_inc(pmax_ready, 1)
                dve.wait_ge(pmax_turned, j + 1)
                own.run(V.tensor_reduce(cmax[0:n, :], ps[0:n, 3, 0:P], AX_X, ALU.max))
                V.tensor_scalar(cmax_b[0:n, :], cmax[0:n, 0:1].broadcast_to([n, P]), 1e-30, None, ALU.max)\
                    .then_inc(cmax_ready, 1)
                dve.wait_ge(cmax_spread, j + 1)
                a, b = cols
                own.run(V.tensor_scalar(p2[:, a:b].bitcast(I32), ps[:, 3, 256:256 + n].bitcast(I32),
                                        0x7F800000, None, ALU.bitwise_and))
                own.run(V.reciprocal(s_w[:, a:b], p2[:, a:b]))
                w_exp = W_EXP if j < JOBS - 1 else F_EXP
                own.run(V.tensor_scalar(s_w[:, a:b], s_w[:, a:b],
                                        2.0 ** (w_exp if j < JOBS - 1 else w_exp + CODE_EXP), None,
                                        ALU.mult))
                last = V.tensor_scalar(undo[:, a:b], p2[:, a:b], 2.0 ** -(w_exp + X_EXP), None, ALU.mult)
                if j == 5:
                    own.run(last)
                    own.run(V.scalar_tensor_tensor(undo_out[:, :], p2[:, 2:3], 2.0 ** (-Y_EXP - W_EXP),
                                                   p2[:, 5:6], ALU.mult, ALU.mult))
                    last = V.tensor_scalar(s_y[:, :], s_w[:, 2:3], 2.0 ** (Y_EXP - W_EXP), None, ALU.mult)
                if j == 6:
                    own.run(last)
                    own.run(V.tensor_scalar(tanh_in[:, :], undo[:, 6:7], GELU_C, None, ALU.mult))
                    own.run(V.scalar_tensor_tensor(undo_down[:, :], p2[:, 6:7], 2.0 ** (-I_EXP - F_EXP),
                                                   p2[:, 7:8], ALU.mult, ALU.mult))
                    last = V.tensor_tensor(undo_down[:, :], undo_down[:, :], p2[:, 8:9], ALU.mult)
                last.then_inc(scale_ready, 1)

            def split_lo(j):
                dve.wait_ge(w_hi_done, j + 1)
                src = stage[:, j % 2, :]
                if j < SECTIONS:
                    hi, lo = (win[:, s, :, j * D:(j + 1) * D] for s in range(2))
                    src = src.rearrange("p (k m) -> p k m", k=KT)
                else:
                    hi, lo = (wout[:, s, :, :].rearrange("p c m -> p (c m)") for s in range(2))
                V.scalar_tensor_tensor(lo, src, s_w[:, j:j + 1], hi, ALU.mult, ALU.subtract)\
                    .then_inc(w_done, 1)

            def norm(n, t):
                for b in range(BLOCKS):
                    if isinstance(n, int) and n < TILES:
                        dve.wait_ge(h_copied, BLOCKS * t + b + 1)
                    own.mark(V.bn_stats(stats[:, b, :], h[:, t * BLOCKS + b, :]))
                own.settle()
                for b in range(BLOCKS):
                    last = V.bn_aggr(mv[:, b, :], stats[:, b, :])
                    if b < BLOCKS - 1:
                        own.mark(last)
                last.then_inc(var_ready, 1)
                dve.wait_ge(std_ready, n + 1)
                own.run(V.reciprocal(rstd[:, :], rstd[:, :]))
                own.run(V.tensor_scalar(rstd[:, :], rstd[:, :], 2.0 ** X_EXP, None, ALU.mult))
                for b in range(BLOCKS):
                    V.tensor_scalar(xn[:, b, :], h[:, t * BLOCKS + b, :], mv[:, b, 0:1], rstd[:, b:b + 1],
                                    ALU.subtract, ALU.mult).then_inc(xn_ready, 1)
                for k in range(KT):
                    dve.wait_ge(x_hi_done, KT * n + k + 1)
                    V.tensor_tensor(xT[:, 1, k, tile_cols(t)], ps[:, 4 + k, :], xT[:, 0, k, tile_cols(t)],
                                    ALU.subtract).then_inc(x_done, 1)

            def y_lo(t, c):
                dve.wait_ge(y_hi_done, CT * t + c + 1)
                V.scalar_tensor_tensor(y_hl[:, 1, c, :], sg[:, c % 2, :], s_y[:, 0:1], y_hl[:, 0, c, :],
                                       ALU.mult, ALU.subtract).then_inc(y_done, 1)

            def unit(t, c):
                u, b = CT * t + c, c % 2
                dve.wait_ge(k_tanh, u + 1)
                dve.wait_ge(v_copied, u + 1)
                own.mark(V.tensor_tensor(tk[:, b, :], tk[:, b, :], vs[:, b, :], ALU.mult))
                dve.wait_ge(a_sig, u + 1)
                a, w = sa[:, b, :], tk[:, b, :]
                own.run(V.tensor_scalar(starts[:, ::CHUNK], sa[:, b, ::CHUNK], A_LO, A_HI, ALU.max, ALU.min))
                own.run(V.tensor_scalar(a, a, A_LO, A_HI, ALU.max, ALU.min))
                own.run(V.memset(sa[:, b, ::SEQ_LEN], 0.0))
                own.run(V.tensor_tensor_scan(mem[:, :], a, starts[:, :], 0.0, ALU.mult, ALU.max))
                own.run(V.tensor_scalar(mem[:, :], mem[:, :], 1.0 / PREFIX_LO, 1.0, ALU.mult, ALU.min))
                own.run(V.tensor_tensor(w, mem[:, :], w, ALU.mult))
                own.run(V.tensor_tensor_scan(mem[:, :], a, w, 0.0, ALU.mult, ALU.add))
                if c == 0:
                    for i in range(CT):
                        dve.wait_ge(rinv_spread, CT * t + i + 1)
                        V.tensor_tensor(qs[:, i, :], qs[:, i, :], ps[:, 4 + i, :], ALU.mult)\
                            .then_inc(q_normed, 1)
                    dve.wait_ge(q_normed, CT * t + CT)
                own.run(V.tensor_tensor(mem[:, :], mem[:, :], qs[:, c, :], ALU.mult))
                own.run(V.tensor_tensor(mem[:, :], mem[:, :], vs[:, b, :], ALU.subtract))
                dve.wait_ge(g_sig, u + 1)
                own.run(V.tensor_tensor(sg[:, b, :], sg[:, b, :], mem[:, :], ALU.mult))
                V.tensor_tensor(sg[:, b, :], sg[:, b, :], vs[:, b, :], ALU.add).then_inc(y_ready, 1)

            def dequantise(n, slot, par, m, half, in_slot):
                raw = stage[:, slot, half * 512:(half + 1) * 512].bitcast(I32)
                scl = stage[:, slot, WORDS + half * 512:WORDS + (half + 1) * 512]
                dve.wait_ge(raw_in[slot], 32 * (in_slot + 1))
                own.run(V.scalar_tensor_tensor(raw, raw, 12, raw, ALU.logical_shift_left, ALU.bitwise_or))
                own.run(V.tensor_scalar(mag[:, :], raw, 0x00070007, 9, ALU.bitwise_and,
                                        ALU.logical_shift_left))
                own.run(V.tensor_scalar(raw, raw, 0x00080008, 12, ALU.bitwise_and, ALU.logical_shift_left))
                own.run(V.tensor_tensor(raw, raw, mag[:, :], ALU.bitwise_or))
                val = stage[:, slot, half * 512:(half + 1) * 512].bitcast(F16)
                for i in range(2):
                    k = 4 * n + 2 * half + i
                    if not (isinstance(k, int) and k < 2):
                        dve.wait_ge(f_done, k - 1)
                    if m < 2:
                        v = val[:, 512 * i:512 * (i + 1)].rearrange("p (w k) -> p k w", k=2)
                        s = scl[:, 256 * i:256 * (i + 1)].unsqueeze(1).broadcast_to([P, 2, 256])
                        o = wf[:, i, :].rearrange("p (k w) -> p k w", k=2)
                    else:
                        v = val.rearrange("p (w k) -> p k w", k=2)[:, i, :]
                        s, o = scl, wf[:, i, :]
                    V.scalar_tensor_tensor(o, v, s_ffn[:, m:m + 1], s, ALU.mult, ALU.mult)\
                        .then_inc(wf_ready, 1)

            def attention(t, first=False, last=False):
                dve.wait_ge(sum_rooted, t + 1)
                V.reciprocal(rinv[:, :], rinv[:, :]).then_inc(rinv_ready, 1)
                for c in range(CT):
                    unit(t, c)
                    if c > 0:
                        y_lo(t, c - 1)
                    if last and c > 0:
                        for half in range(2):
                            m = c - 1
                            dequantise(m, load_slot(m), 0, m, half, m // 2)
                y_lo(t, CT - 1)
                for b in range(BLOCKS):
                    dve.wait_ge(attn_out, BLOCKS * t + b + 1)
                    bank = (6, 7, 4, 5)[b]
                    blk = h[:, t * BLOCKS + b, :]
                    V.scalar_tensor_tensor(blk, ps[:, bank, :], undo_out[:, 0:1], blk, ALU.mult, ALU.add)\
                        .then_inc(attn_added, 1)
                dve.wait_ge(attn_added, BLOCKS * t + BLOCKS)
                own.run(V.memset(stats[:, :, :], 0.0))
                norm(TILES + t, t)
                own.restart()

            def add_down(tile_index, t):
                for b in range(BLOCKS):
                    dve.wait_ge(down_made, BLOCKS * tile_index + b + 1)
                    blk = h[:, t * BLOCKS + b, :]
                    V.scalar_tensor_tensor(blk, ps[:, b, :], undo_down[:, 0:1], blk, ALU.mult, ALU.add)\
                        .then_inc(down_free, 1)

            def ffn_group(group, par, pair, last=False, first=False):
                for s in range(STEPS):
                    index, b = STEPS * group + s, s % 2
                    gate, up = ps[:, 4 + 2 * b, :], ps[:, 5 + 2 * b, :]
                    dve.wait_ge(gate_squared, index + 1)
                    own.run(V.tensor_scalar(sq[:, b, :], sq[:, b, :], GELU_A, 1.0, ALU.mult, ALU.add))
                    V.tensor_tensor(sq[:, b, :], sq[:, b, :], gate, ALU.mult).then_inc(inner_ready, 1)
                    if s >= 2 and s % 2 == 0 and s <= 12 and not last:
                        piece = (s - 2) // 2
                        m, half = piece // 2, piece % 2
                        n = 6 * pair + 3 * (par + 1) + m
                        dequantise(n, (par + 1 + m) % 2, 1 - par, m, half,
                                   3 * pair + (3 * (par + 1) + m) // 2)
                    dve.wait_ge(tanh_done, index + 1)
                    own.run(V.scalar_tensor_tensor(th[:, b, :], th[:, b, :], 1.0, gate, ALU.add, ALU.mult))
                    dve.wait_ge(up_made, index + 1)
                    V.scalar_tensor_tensor(th[:, b, :], th[:, b, :],
                                           0.5 * 2.0 ** (I_EXP - 2 * (F_EXP + X_EXP)), up,
                                           ALU.mult, ALU.mult).then_inc(inter_ready, 1)
                    dve.wait_ge(inter_hi, index + 1)
                    V.tensor_tensor(inter[:, b, 1, :], th[:, b, :], inter[:, b, 0, :], ALU.subtract)\
                        .then_inc(inter_done, 1)
                    if s % GROUP == 0 and not (first and s == 0):
                        add_down(TILES * group + s // GROUP - 1, (s // GROUP - 1) % TILES)
                own.restart()

            s_ffn = s_w[:, 6:9]
            dve.wait_ge(ids_in, 16)
            own.run(V.tensor_scalar(ids_f[:, 0, :], ids_sb[:, :], 0.0, float(VOCAB), ALU.is_lt, ALU.mult))
            own.run(V.tensor_tensor(ids_f[:, 1, :], ids_f[:, 0, :], ids_sb[:, :], ALU.add))
            V.tensor_scalar(rows[:, :], ids_f[:, 1, :], 0.0, float(VOCAB - 1), ALU.max, ALU.min)\
                .then_inc(rows_ready, 1)
            own.mark(V.memset(starts[:, :], 0.0))
            for t in range(TILES):
                scale_of(t, (t, t + 1))
                split_lo(t)
                norm(t, t)
            scale_of(4, (4, 5))
            split_lo(4)
            scale_of(5, (5, 6))
            split_lo(5)
            scale_of(6, (6, 9))
            own.restart()
            attention(0)
            with dve.Fori(1, TILES - 1) as t:
                attention(t)
            attention(TILES - 1, last=True)
            dve.sem_inc(down_free, BLOCKS)
            ffn_group(0, 0, 0, first=True)
            ffn_group(1, 1, 0)
            with dve.Fori(1, PAIRS - 1) as pair:
                ffn_group(2 * pair, 0, pair)
                ffn_group(2 * pair + 1, 1, pair)
            ffn_group(GROUPS - 2, 0, PAIRS - 1)
            ffn_group(GROUPS - 1, 1, PAIRS - 1, last=True)
            add_down(TILES * GROUPS - 1, TILES - 1)


def kernel(x, L0_tok_E, L0_tok_P, L0_attn_w_in, L0_attn_w_out, L0_ffn_gate_W_packed, L0_ffn_gate_scales,
           L0_ffn_up_W_packed, L0_ffn_up_scales, L0_ffn_down_W_packed, L0_ffn_down_scales):
    import numpy as np
    import concourse.bacc as bacc
    from concourse.bass_utils import run_bass_kernel_spmd

    def array(a):
        return np.asarray(a)

    def rows_by_channel(w):
        m = w.shape[0]
        return w.reshape(m, 2, P, 2).transpose(2, 3, 1, 0).reshape(P, KT, m)

    def up_words(w):
        return w.reshape(GROUPS, 2, P, 2, 2, P).transpose(0, 5, 1, 3, 4, 2).reshape(GROUPS, P, WORDS)

    def up_scales(w):
        return w.reshape(GROUPS, 2, P, 2, 2, 8).transpose(0, 5, 1, 3, 4, 2).reshape(GROUPS, 8, WORDS)

    def down_words(w):
        return w.reshape(D, GROUPS, 2, P).transpose(1, 3, 2, 0).reshape(GROUPS, P, WORDS)

    def down_scales(w):
        return w.reshape(D, GROUPS, 2, 8).transpose(1, 3, 2, 0).reshape(GROUPS, 8, WORDS)

    gate_s, up_s, down_s = (array(a) for a in (L0_ffn_gate_scales, L0_ffn_up_scales, L0_ffn_down_scales))
    w_in = rows_by_channel(array(L0_attn_w_in))
    arrays = {
        "ids": array(x).T,
        "table": array(L0_tok_E),
        "p_t": array(L0_tok_P).T,
        "w_in": w_in.reshape(P, KT, SECTIONS, D).transpose(2, 0, 1, 3).reshape(SECTIONS, P, KT * D),
        "w_out": array(L0_attn_w_out).T.reshape(CT, P, D).transpose(1, 0, 2).reshape(P, CT * D),
        "all_scales": np.concatenate([a.reshape(P, 512) for a in (gate_s, up_s, down_s)], axis=1),
        "packed": np.stack([up_words(array(L0_ffn_gate_W_packed)), up_words(array(L0_ffn_up_W_packed)),
                            down_words(array(L0_ffn_down_W_packed))], axis=1).reshape(3 * GROUPS, P, WORDS),
        "scales": np.stack([up_scales(gate_s), up_scales(up_s), down_scales(down_s)],
                           axis=1).reshape(3 * GROUPS, 8, WORDS),
    }
    arrays = {k: np.ascontiguousarray(v) for k, v in arrays.items()}
    nc = bacc.Bacc("TRN2", target_bir_lowering=False, num_devices=1)
    aps = [nc.dram_tensor(k, v.shape, mybir.dt.from_np(v.dtype), kind="ExternalInput").ap()
           for k, v in arrays.items()]
    out = nc.dram_tensor("out", (SEQS, SEQ_LEN, D), F32, kind="ExternalOutput").ap()
    lm_layer(nc, *aps, out.rearrange("s p d -> p s d"))
    result = run_bass_kernel_spmd(nc, [arrays], core_ids=[0])
    return result.results[0]["out"]
```

```python
from contextlib import ExitStack

import concourse.bass as bass
from concourse import mybir

F32 = mybir.dt.float32
F16 = mybir.dt.float16
I32 = mybir.dt.int32
U32 = mybir.dt.uint32
ALU = mybir.AluOpType
ACT = mybir.ActivationFunctionType
AX_X = mybir.AxisListType.X

P = 128
SEQS, SEQ_LEN = 16, 128
VOCAB, D_EMBED, D = 32000, 128, 512
MLP = 4096
HEADS, HEAD_DIM, CHUNK = 16, 32, 64
TOKENS = SEQS * SEQ_LEN
TILE = 512
TILES = TOKENS // TILE
BLOCKS = TILE // P
KT = D // P
CT = D // P
SECTIONS = 5
RMS_EPS, LN_EPS = 1.1920928955078125e-07, 1e-05
A_LO, A_HI, PREFIX_LO = 0.6, 0.9995, 1e-06
BLK = 32
GROUP = 4
GROUPS = MLP // (GROUP * P)
PAIRS = GROUPS // 2
STEPS = TILES * GROUP
WORDS = 1024

W_EXP = 14
F_EXP = 12
CODE_EXP = 14
X_EXP = 11
Y_EXP = -5
I_EXP = -11
GELU_A, GELU_C = 0.044715, 0.7978845608028654

JOBS = 7
MAXES = 9


class Steps:

    def __init__(self, eng, sem):
        self.eng, self.sem, self.n = eng, sem, 0

    def mark(self, instruction):
        instruction.then_inc(self.sem, 1)
        self.n += 1

    def settle(self):
        self.eng.wait_ge(self.sem, self.n)

    def run(self, instruction):
        self.mark(instruction)
        self.settle()

    def restart(self):
        self.settle()
        self.eng.sem_clear(self.sem)
        self.n = 0


def lm_layer(nc, ids, table, p_t, w_in, w_out, all_scales, packed, scales, out):
    with ExitStack() as ctx:
        def sb(name, shape, dt):
            return ctx.enter_context(nc.sbuf_tensor(name, shape, dt))

        def sem(name):
            return ctx.enter_context(nc.semaphore(name))

        h = sb("h", [P, SEQS, D], F32)
        xT = sb("xT", [P, 2, KT, TOKENS], F16)
        region = sb("region", [P, 10240], F32)
        win = region[:, :].bitcast(F16).rearrange("p (s k m) -> p s k m", s=2, k=KT)
        wout = sb("wout", [P, 2, CT, D], F16)
        even_w = sb("even_w", [P, 3, 2, GROUP, D], F16)
        odd_w = region[:, 0:6144].bitcast(F16).rearrange("p (m s n w) -> p m s n w", s=2, m=3, n=GROUP)
        ffn_w = [even_w, odd_w]
        sq = region[:, 6144:7168].rearrange("p (b t) -> p b t", b=2)
        th = region[:, 7168:8192].rearrange("p (b t) -> p b t", b=2)
        inter = region[:, 8192:9216].bitcast(F16).rearrange("p (b s t) -> p b s t", b=2, s=2)
        stage = sb("stage", [P, 2, 2048], F32)
        tk = sb("tk", [P, 2, TILE], F32)
        vs = sb("vs", [P, 2, TILE], F32)
        sa = sb("sa", [P, 2, TILE], F32)
        sg = sb("sg", [P, 2, TILE], F32)
        mem = sb("mem", [P, TILE], F32)
        starts = sb("starts", [P, TILE], F32)
        qs = sb("qs", [P, CT, TILE], F32)
        q2 = sb("q2", [P, 2, TILE], F32)
        yx = sb("yx", [P, 4 * TILE], F32)
        y_hl = yx[:, :].bitcast(F16).rearrange("p (s c t) -> p s c t", s=2, c=CT)
        xn_last = yx[:, :].rearrange("p (b d) -> p b d", b=BLOCKS)
        emb_area = even_w[:, 1, :, :, :].rearrange("p s n w -> p (s n w)").bitcast(F32)
        emb = emb_area[:, 0:1024].rearrange("p (b s e) -> p b s e", b=2, s=BLOCKS)
        emb_t, pt_sb = emb_area[:, 1024:1536], emb_area[:, 1536:2048]
        xn = even_w[:, 2, :, :, :].rearrange("p s n w -> p (s n w)").bitcast(F32)\
            .rearrange("p (b d) -> p b d", b=BLOCKS)
        rinv = sb("rinv", [HEADS, TILE], F32)
        mag = sb("mag", [P, 512], I32)
        wf = sb("wf", [P, 2, 512], F32)
        ident = sb("ident", [P, P], F32)
        head_sum = sb("head_sum", [P, CT, HEADS], F32)
        head_spread = sb("head_spread", [HEADS, D], F32)
        bias = sb("bias", [P, 4], F32)
        ids_sb = sb("ids_sb", [P, SEQS], I32)
        ids_f = sb("ids_f", [P, 2, SEQS], F32)
        rows = sb("rows", [P, SEQS], I32)
        pmax = sb("pmax", [P, MAXES], F32)
        gmax = sb("gmax", [P, MAXES], F32)
        amax = sb("amax", [P, 1], F32)
        p2 = sb("p2", [P, MAXES], F32)
        s_w = sb("s_w", [P, MAXES], F32)
        undo = sb("undo", [P, MAXES], F32)
        s_y = sb("s_y", [P, 1], F32)
        undo_out = sb("undo_out", [P, 1], F32)
        undo_down = sb("undo_down", [P, 1], F32)
        tanh_in = sb("tanh_in", [P, 1], F32)
        stats = sb("stats", [P, BLOCKS, 6], F32)
        mv = sb("mv", [P, BLOCKS, 2], F32)
        rstd = sb("rstd", [P, BLOCKS], F32)
        ps = ctx.enter_context(nc.psum_tensor("ps", [P, 8, TILE], F32))

        ids_in, pt_in, out_stored = sem("ids_in"), sem("pt_in"), sem("out_stored")
        emb_in = [sem(f"emb_in{t}") for t in range(TILES)]
        stage_in = [sem(f"stage_in{s}") for s in range(2)]
        raw_in = [sem(f"raw_in{s}") for s in range(2)]
        consts_ready, rows_ready, zeroed = sem("consts_ready"), sem("rows_ready"), sem("zeroed")
        pmax_ready, gmax_ready = sem("pmax_ready"), sem("gmax_ready")
        scale_ready, w_hi_done, w_done = sem("scale_ready"), sem("w_hi_done"), sem("w_done")
        emb_turned, emb_copied, h_made, h_copied = (
            sem("emb_turned"), sem("emb_copied"), sem("h_made"), sem("h_copied"))
        var_ready, std_ready, xn_ready, x_turned, x_hi_done, x_done = (
            sem("var_ready"), sem("std_ready"), sem("xn_ready"), sem("x_turned"), sem("x_hi_done"),
            sem("x_done"))
        q_made, q_copied, q_squared, sum_made, sum_rooted, rinv_ready, rinv_spread, q_normed = (
            sem("q_made"), sem("q_copied"), sem("q_squared"), sem("sum_made"), sem("sum_rooted"),
            sem("rinv_ready"), sem("rinv_spread"), sem("q_normed"))
        k_made, v_made, a_made, g_made = sem("k_made"), sem("v_made"), sem("a_made"), sem("g_made")
        k_tanh, v_copied, u_ready, a_sig, g_sig = (
            sem("k_tanh"), sem("v_copied"), sem("u_ready"), sem("a_sig"), sem("g_sig"))
        y_ready, y_hi_done, y_done = sem("y_ready"), sem("y_hi_done"), sem("y_done")
        attn_out, attn_added = sem("attn_out"), sem("attn_added")
        wf_ready, f_hi_done, f_done = sem("wf_ready"), sem("f_hi_done"), sem("f_done")
        gate_made, up_made, gate_squared, inner_ready, tanh_done, inter_ready, inter_hi, inter_done = (
            sem("gate_made"), sem("up_made"), sem("gate_squared"), sem("inner_ready"), sem("tanh_done"),
            sem("inter_ready"), sem("inter_hi"), sem("inter_done"))
        down_made, down_added = sem("down_made"), sem("down_added")
        dve_step, pool_step = sem("dve_step"), sem("pool_step")

        block = ctx.enter_context(nc.Block())

        def tile_cols(t):
            return bass.ts(t, TILE)

        def norm_1(t):
            return 2 * t - 1 if not isinstance(t, int) or t > 0 else 0

        def norm_2(t):
            return 2 * t + 2 if not isinstance(t, int) or t < TILES - 1 else 2 * TILES - 1

        def load_slot(n):
            return n % 2

        @block.sync
        def _(sp):
            sp.dma_start(ids_sb[:, :], ids).then_inc(ids_in, 16)
            sp.dma_start(pt_sb, p_t).then_inc(pt_in, 16)
            for j in range(JOBS):
                if j >= 2:
                    sp.wait_ge(w_done, j - 1)
                if j < SECTIONS:
                    src, dst = w_in[j], stage[:, j % 2, :]
                elif j == SECTIONS:
                    src, dst = w_out, stage[:, j % 2, :]
                else:
                    src, dst = all_scales, stage[:, j % 2, 0:1536]
                sp.dma_start(dst, src).then_inc(stage_in[j % 2], 16)

            def load_packed(n, slot):
                sp.dma_start(stage[:, slot, 0:WORDS].bitcast(I32), packed[n]).then_inc(raw_in[slot], 16)
                sp.dma_start(stage[:, slot, WORDS:], scales[n].unsqueeze(1).broadcast_to([8, 16, WORDS]))\
                  .then_inc(raw_in[slot], 16)

            sp.wait_ge(pmax_ready, JOBS)
            load_packed(0, 0)
            load_packed(1, 1)

            def later_loads(pair, count):
                for i in range(count):
                    n = 6 * pair + i + 2
                    sp.wait_ge(wf_ready, 4 * (6 * pair + i + 1))
                    load_packed(n, i % 2)

            with sp.Fori(0, PAIRS - 1) as pair:
                later_loads(pair, 6)
            later_loads(PAIRS - 1, 4)
            for t in range(TILES):
                sp.wait_ge(down_added, BLOCKS * ((GROUPS - 1) * TILES + t + 1))
                sp.dma_start(out[:, t * BLOCKS:(t + 1) * BLOCKS, :], h[:, t * BLOCKS:(t + 1) * BLOCKS, :])\
                  .then_inc(out_stored, 16)
            sp.wait_ge(out_stored, 16 * TILES)

        @block.gpsimd
        def _(pool):
            own = Steps(pool, pool_step)

            def gather(t):
                if t >= 2:
                    pool.wait_ge(emb_turned, t - 1)
                for s in range(BLOCKS):
                    q = BLOCKS * t + s
                    nc.gpsimd.indirect_dma_start(
                        out=emb[:, t % 2, s, :], out_offset=None, in_=table,
                        in_offset=bass.IndirectOffsetOnAxis(ap=rows[:, q:q + 1].bitcast(U32), axis=0),
                    ).then_inc(emb_in[t], 16)

            def max_over_partitions(j):
                a, b = (j, j + 1) if j < JOBS - 1 else (JOBS - 1, MAXES)
                pool.wait_ge(pmax_ready, j + 1)
                nc.gpsimd.partition_all_reduce(gmax[:, a:b], pmax[:, a:b], P,
                                               bass.bass_isa.ReduceOp.max).then_inc(gmax_ready, 1)

            def make_u(t, c):
                u, b = CT * t + c, c % 2
                pool.wait_ge(k_tanh, u + 1)
                pool.wait_ge(v_copied, u + 1)
                nc.gpsimd.tensor_tensor(tk[:, b, :], tk[:, b, :], vs[:, b, :], ALU.mult)\
                    .then_inc(u_ready, 1)

            pool.wait_ge(rows_ready, 1)
            gather(0)
            own.mark(nc.gpsimd.memset(ident[:, :], 0.0))
            own.mark(nc.gpsimd.memset(head_sum[:, :, :], 1.0))
            own.mark(nc.gpsimd.memset(head_spread[:, :], 1.0))
            own.mark(nc.gpsimd.memset(bias[:, 0:1], 2.0))
            own.mark(nc.gpsimd.memset(bias[:, 1:2], RMS_EPS))
            own.mark(nc.gpsimd.memset(bias[:, 2:3], LN_EPS))
            own.settle()
            nc.gpsimd.affine_select(out=ident[:, :], in_=ident[:, :], compare_op=ALU.not_equal,
                                    fill=1.0, base=0, pattern=[[-1, P]], channel_multiplier=1)\
                .then_inc(consts_ready, 1)
            max_over_partitions(0)
            max_over_partitions(1)
            hs = head_sum[:, :, :]
            own.run(nc.gpsimd.affine_select(out=hs, in_=hs, compare_op=ALU.is_ge, fill=0.0, base=0,
                                            pattern=[[P, CT], [-HEAD_DIM, HEADS]], channel_multiplier=1))
            own.run(nc.gpsimd.affine_select(out=hs, in_=hs, compare_op=ALU.is_ge, fill=0.0,
                                            base=HEAD_DIM - 1, pattern=[[-P, CT], [HEAD_DIM, HEADS]],
                                            channel_multiplier=-1))
            hp = head_spread[:, :]
            own.run(nc.gpsimd.affine_select(out=hp, in_=hp, compare_op=ALU.is_ge, fill=0.0, base=0,
                                            pattern=[[1, D]], channel_multiplier=-HEAD_DIM))
            nc.gpsimd.affine_select(out=hp, in_=hp, compare_op=ALU.is_ge, fill=0.0,
                                    base=HEAD_DIM - 1, pattern=[[-1, D]],
                                    channel_multiplier=HEAD_DIM).then_inc(consts_ready, 1)
            gather(1)
            max_over_partitions(2)
            gather(2)
            max_over_partitions(3)

            def f_lo(n, par, m, half):
                for i in range(2):
                    k = 4 * n + 2 * half + i
                    pool.wait_ge(f_hi_done, k + 1)
                    nc.gpsimd.tensor_tensor(ffn_w[par][:, m, 1, 2 * half + i, :], wf[:, i, :],
                                            ffn_w[par][:, m, 0, 2 * half + i, :],
                                            ALU.subtract).then_inc(f_done, 1)

            def group_lo(n0, par):
                for m in range(3):
                    for half in range(2):
                        f_lo(n0 + m, par, m, half)

            for c in range(CT):
                make_u(0, c)
                if c < 3:
                    max_over_partitions(4 + c)
            gather(3)
            with pool.Fori(1, TILES - 1) as t:
                for c in range(CT):
                    make_u(t, c)
            for c in range(CT):
                make_u(TILES - 1, c)
                if c > 0:
                    f_lo(c - 1, 0, c - 1, 0)
                    f_lo(c - 1, 0, c - 1, 1)
            group_lo(3, 1)
            with pool.Fori(1, PAIRS) as pair:
                group_lo(6 * pair, 0)
                group_lo(6 * pair + 3, 1)

        @block.scalar
        def _(act):
            def split_hi(j):
                act.wait_ge(scale_ready, j + 1)
                src = stage[:, j % 2, :]
                if j < SECTIONS:
                    dst = win[:, 0, :, j * D:(j + 1) * D]
                    src = src.rearrange("p (k m) -> p k m", k=KT)
                else:
                    dst = wout[:, 0, :, :].rearrange("p c m -> p (c m)")
                nc.scalar.activation(dst, src, ACT.Identity, scale=s_w[:, j:j + 1]).then_inc(w_hi_done, 1)

            def deviation(n):
                act.wait_ge(var_ready, n + 1)
                nc.scalar.activation(rstd[:, :], mv[:, :, 1], ACT.Sqrt, bias=bias[:, 2:3])\
                    .then_inc(std_ready, 1)

            def x_hi(n, t, bank=4):
                for k in range(KT):
                    act.wait_ge(x_turned, KT * n + k + 1)
                    nc.scalar.activation(xT[:, 0, k, tile_cols(t)], ps[:, bank + k, :], ACT.Copy)\
                        .then_inc(x_hi_done, 1)

            def copy_emb(t):
                act.wait_ge(emb_turned, t + 1)
                nc.scalar.activation(emb_t, ps[:, 4, :], ACT.Copy).then_inc(emb_copied, 1)

            def copy_h(t):
                for b in range(BLOCKS):
                    act.wait_ge(h_made, BLOCKS * t + b + 1)
                    nc.scalar.activation(h[:, BLOCKS * t + b, :], ps[:, (5, 6, 7, 4)[b], :], ACT.Copy)\
                        .then_inc(h_copied, 1)

            def copy_q(t, c):
                act.wait_ge(q_made, CT * t + c + 1)
                nc.scalar.activation(qs[:, c, :], ps[:, 4 + c, :], ACT.Identity, scale=undo[:, 0:1])\
                    .then_inc(q_copied, 1)

            def square_q(t, c, waits=True):
                act.wait_ge(q_copied, CT * t + c + 1)
                if c >= 2:
                    act.wait_ge(sum_made, CT * t + c - 1)
                nc.scalar.activation(q2[:, c % 2, :], qs[:, c, :], ACT.Square).then_inc(q_squared, 1)

            def root_sums(t):
                act.wait_ge(sum_made, CT * t + CT)
                nc.scalar.activation(rinv[:, :], ps[0:HEADS, 4, :], ACT.Sqrt, bias=bias[0:HEADS, 1:2],
                                     scale=1.0 / HEAD_DIM).then_inc(sum_rooted, 1)

            def unit(t, c, first=False, after_k=None, after_v=None):
                u, b, col = CT * t + c, c % 2, slice(1 + c, 2 + c)
                if not (first and c < 2):
                    act.wait_ge(y_ready, u - 1)
                act.wait_ge(k_made, u + 1)
                nc.scalar.activation(tk[:, b, :], ps[:, 0, :], ACT.Tanh, scale=undo[:, col])\
                    .then_inc(k_tanh, 1)
                if after_k:
                    after_k()
                act.wait_ge(v_made, u + 1)
                nc.scalar.activation(vs[:, b, :], ps[:, 1, :], ACT.Identity, scale=undo[:, col])\
                    .then_inc(v_copied, 1)
                if after_v:
                    after_v()
                act.wait_ge(a_made, u + 1)
                nc.scalar.activation(sa[:, b, :], ps[:, 2, :], ACT.Sigmoid, bias=bias[:, 0:1],
                                     scale=undo[:, col]).then_inc(a_sig, 1)
                if not (first and c < 2):
                    act.wait_ge(y_done, u - 1)
                act.wait_ge(g_made, u + 1)
                nc.scalar.activation(sg[:, b, :], ps[:, 3, :], ACT.Sigmoid, scale=undo[:, col])\
                    .then_inc(g_sig, 1)

            def y_hi(t, c):
                act.wait_ge(y_ready, CT * t + c + 1)
                nc.scalar.activation(y_hl[:, 0, c, :], sg[:, c % 2, :], ACT.Identity, scale=s_y[:, 0:1])\
                    .then_inc(y_hi_done, 1)

            def f_hi(n, par, m, half):
                for i in range(2):
                    act.wait_ge(wf_ready, 4 * n + 2 * half + i + 1)
                    nc.scalar.activation(ffn_w[par][:, m, 0, 2 * half + i, :], wf[:, i, :], ACT.Copy)\
                        .then_inc(f_hi_done, 1)

            def attention(t, first=False, last=False):
                unit(t, 0, first)
                if first:
                    split_hi(4)
                unit(t, 1, first)
                y_hi(t, 0)
                if first:
                    split_hi(5)
                else:
                    x_hi(norm_2(t - 1), t - 1)
                if last:
                    f_hi(0, 0, 0, 0)
                    f_hi(0, 0, 0, 1)
                    unit(t, 2)
                    y_hi(t, 1)
                    f_hi(1, 0, 1, 0)
                    f_hi(1, 0, 1, 1)
                    unit(t, 3)
                    y_hi(t, 2)
                    y_hi(t, 3)
                    f_hi(2, 0, 2, 0)
                    f_hi(2, 0, 2, 1)
                    deviation(norm_2(t))
                    x_hi(norm_2(t), t, 0)
                    return
                unit(t, 2, first, lambda: copy_emb(t + 1), lambda: copy_h(t + 1))
                deviation(norm_1(t + 1))
                y_hi(t, 1)
                unit(t, 3, first, None, lambda: x_hi(norm_1(t + 1), t + 1))
                y_hi(t, 2)
                for c in range(2):
                    copy_q(t + 1, c)
                for c in range(2):
                    square_q(t + 1, c)
                copy_q(t + 1, 2)
                y_hi(t, 3)
                copy_q(t + 1, 3)
                for c in range(2, CT):
                    square_q(t + 1, c)
                root_sums(t + 1)
                deviation(norm_2(t))

            def ffn_step(s, index):
                b = s % 2
                act.wait_ge(gate_made, index + 1)
                nc.scalar.activation(sq[:, b, :], ps[:, 4 + 2 * b, :], ACT.Square, scale=undo[:, 6:7])\
                    .then_inc(gate_squared, 1)
                act.wait_ge(inner_ready, index + 1)
                nc.scalar.activation(th[:, b, :], sq[:, b, :], ACT.Tanh, scale=tanh_in[:, 0:1])\
                    .then_inc(tanh_done, 1)

            def inter_high(s, index):
                act.wait_ge(inter_ready, index + 1)
                nc.scalar.activation(inter[:, s % 2, 0, :], th[:, s % 2, :], ACT.Copy).then_inc(inter_hi, 1)

            def ffn_group(group, par, last=False):
                for s in range(STEPS):
                    index = STEPS * group + s
                    ffn_step(s, index)
                    if s >= 2 and s % 2 == 0 and s <= 12 and not last:
                        piece = (s - 2) // 2
                        f_hi(3 * (group + 1) + piece // 2, 1 - par, piece // 2, piece % 2)
                    inter_high(s, index)

            act.wait_ge(consts_ready, 1)
            split_hi(0)
            copy_emb(0)
            copy_h(0)
            deviation(0)
            split_hi(1)
            x_hi(0, 0)
            copy_q(0, 0)
            copy_q(0, 1)
            split_hi(2)
            square_q(0, 0)
            square_q(0, 1)
            copy_q(0, 2)
            copy_q(0, 3)
            split_hi(3)
            square_q(0, 2)
            square_q(0, 3)
            root_sums(0)
            attention(0, first=True)
            with act.Fori(1, TILES - 1) as t:
                attention(t)
            attention(TILES - 1, last=True)
            act.wait_ge(scale_ready, JOBS)
            with act.Fori(0, PAIRS - 1) as pair:
                ffn_group(2 * pair, 0)
                ffn_group(2 * pair + 1, 1)
            ffn_group(GROUPS - 2, 0)
            ffn_group(GROUPS - 1, 1, last=True)

        @block.tensor
        def _(pe):
            def products(dst, terms, sem_done=None, n=1):
                for i, (w, x) in enumerate(terms):
                    last = nc.tensor.matmul(dst, w, x, start=(i == 0), stop=(i == len(terms) - 1))
                if sem_done is not None:
                    last.then_inc(sem_done, n)

            def in_terms(sec, c, t):
                at = c * P if sec == 0 else (1 + c) * D + (sec - 1) * P
                cols = slice(at, at + P)
                return [(win[:, a, k, cols], xT[:, b, k, tile_cols(t)])
                        for k in range(KT) for a, b in ((0, 0), (0, 1), (1, 0))]

            def turn_tokens(n, src_of=xn, bank=4):
                pe.wait_ge(xn_ready, BLOCKS * n + BLOCKS)
                for k in range(KT):
                    nib, half = k // 2, k % 2
                    for b in range(BLOCKS):
                        src = src_of[:, b, 256 * half:256 * half + 256].rearrange("p (m i) -> p i m", i=2)
                        last = nc.tensor.transpose(ps[:, bank + k, b * P:(b + 1) * P], src[:, nib, :],
                                                   ident[:, :])
                    last.then_inc(x_turned, 1)

            def turn_emb(t, b_of):
                for b in range(BLOCKS):
                    last = nc.tensor.transpose(ps[:, 4, b * P:(b + 1) * P], emb[:, b_of, b, :], ident[:, :])
                last.then_inc(emb_turned, 1)

            def make_h(t):
                pe.wait_ge(emb_copied, t + 1)
                for b in range(BLOCKS):
                    nc.tensor.matmul(ps[:, (5, 6, 7, 4)[b], :], emb_t[:, b * P:(b + 1) * P], pt_sb,
                                     start=True, stop=True).then_inc(h_made, 1)

            def make_q(t, c):
                products(ps[:, 4 + c, :], in_terms(0, c, t), q_made)

            def sum_squares(t, c):
                pe.wait_ge(q_squared, CT * t + c + 1)
                nc.tensor.matmul(ps[0:HEADS, 4, :], head_sum[:, c, :], q2[:, c % 2, :], start=(c == 0),
                                 stop=(c == CT - 1)).then_inc(sum_made, 1)

            def spread_rinv(t):
                pe.wait_ge(rinv_ready, t + 1)
                for c in range(CT):
                    nc.tensor.matmul(ps[:, 4 + c, :], head_spread[:, c * P:(c + 1) * P], rinv[:, :],
                                     start=True, stop=True).then_inc(rinv_spread, 1)

            def unit(t, c, first=False, after_v=None, after_k=None):
                u = CT * t + c
                if first:
                    pe.wait_ge(w_done, c + 2)
                for i, (made, read) in enumerate(((k_made, k_tanh), (v_made, v_copied), (a_made, a_sig),
                                                  (g_made, g_sig))):
                    if not (first and c == 0):
                        pe.wait_ge(read, u)
                    if not first and c == 0:
                        pe.wait_ge(attn_added, BLOCKS * (t - 1) + i + 1)
                    products(ps[:, i, :], in_terms(1 + i, c, t), made)
                    if i == 0 and after_k:
                        after_k()
                    if i == 1 and after_v:
                        after_v()

            def project(t, b, bank):
                products(ps[:, bank, :],
                         [(y_hl[:, x, c, b * P:(b + 1) * P], wout[:, w, c, :])
                          for c in range(CT) for x, w in ((0, 0), (0, 1), (1, 0))], attn_out)

            def attention(t, parity=0, first=False, last=False):
                unit(t, 0, first)
                pe.wait_ge(q_copied, CT * t + CT)
                spread_rinv(t)
                unit(t, 1, first)
                pe.wait_ge(q_normed, CT * t + CT)
                if not first:
                    turn_tokens(norm_2(t - 1))

                def next_emb():
                    pe.wait_ge(emb_in[t + 1], 16 * BLOCKS)
                    if not first:
                        pe.wait_ge(x_done, KT * (norm_2(t - 1) + 1))
                    turn_emb(t + 1, parity)

                if last:
                    unit(t, 2)
                    unit(t, 3)
                    pe.wait_ge(f_done, 8)
                    gate_up(0, 0, 0)
                    for i, read in enumerate((k_tanh, v_copied, a_sig, g_sig)):
                        pe.wait_ge(read, CT * t + CT)
                    pe.wait_ge(y_done, CT * t + CT)
                    for b in range(BLOCKS):
                        project(t, b, b)
                    gate_up(1, 0, 0)
                    pe.wait_ge(attn_added, BLOCKS * t + BLOCKS)
                    turn_tokens(norm_2(t), xn_last, 0)
                    return
                unit(t, 2, first, after_k=next_emb, after_v=lambda: make_h(t + 1))

                def next_turn():
                    pe.wait_ge(h_copied, BLOCKS * (t + 1) + BLOCKS)
                    turn_tokens(norm_1(t + 1))

                unit(t, 3, first, after_v=next_turn)
                pe.wait_ge(x_done, KT * (norm_1(t + 1) + 1))
                for c in range(CT):
                    make_q(t + 1, c)
                pe.wait_ge(q_copied, CT * (t + 1) + 1)
                for c in range(CT):
                    sum_squares(t + 1, c)
                pe.wait_ge(y_done, CT * t + CT)
                pe.wait_ge(g_sig, CT * t + CT)
                for b in range(BLOCKS):
                    project(t, b, b)

            def gate_up(s, par, t):
                ni, b = s % GROUP, s % 2
                for m, made in ((0, gate_made), (1, up_made)):
                    products(ps[:, 4 + 2 * b + m, :],
                             [(ffn_w[par][:, m, w, ni, k * P:(k + 1) * P], xT[:, x, k, tile_cols(t)])
                              for k in range(KT) for w, x in ((0, 0), (0, 1), (1, 0))], made)

            def down(s, par, index, tile_index):
                ni = s % GROUP
                if ni == 0 and not (isinstance(tile_index, int) and tile_index == 0):
                    pe.wait_ge(down_added, BLOCKS * tile_index)
                pe.wait_ge(inter_done, index + 1)
                for b in range(BLOCKS):
                    for i, (x, w) in enumerate(((0, 0), (0, 1), (1, 0))):
                        last = nc.tensor.matmul(ps[:, b, :], inter[:, s % 2, x, b * P:(b + 1) * P],
                                                ffn_w[par][:, 2, w, ni, :],
                                                start=(ni == 0 and i == 0), stop=(ni == GROUP - 1 and i == 2))
                    if ni == GROUP - 1:
                        last.then_inc(down_made, 1)

            def ffn_group(group, par, last=False, first=False):
                for s in range(STEPS):
                    if first and s == 0:
                        pe.wait_ge(x_done, 2 * KT * TILES)
                        pe.wait_ge(f_done, 12)
                    elif s + 1 < STEPS:
                        gate_up(s + 1, par, (s + 1) // GROUP)
                    elif not last:
                        pe.wait_ge(f_done, 12 * (group + 2))
                        gate_up(0, 1 - par, 0)
                    down(s, par, STEPS * group + s, TILES * group + s // GROUP)

            pe.wait_ge(consts_ready, 1)
            pe.wait_ge(emb_in[0], 16 * BLOCKS)
            turn_emb(0, 0)
            pe.wait_ge(pt_in, 16)
            make_h(0)
            pe.wait_ge(h_copied, BLOCKS)
            turn_tokens(0)
            pe.wait_ge(w_done, 1)
            pe.wait_ge(x_done, KT)
            for c in range(CT):
                make_q(0, c)
            pe.wait_ge(consts_ready, 2)
            pe.wait_ge(q_copied, 1)
            for c in range(CT):
                sum_squares(0, c)
            attention(0, 1, first=True)
            attention(1, 0)
            attention(2, 1)
            attention(TILES - 1, last=True)
            ffn_group(0, 0, first=True)
            ffn_group(1, 1)
            with pe.Fori(1, PAIRS - 1) as pair:
                ffn_group(2 * pair, 0)
                ffn_group(2 * pair + 1, 1)
            ffn_group(GROUPS - 2, 0)
            ffn_group(GROUPS - 1, 1, last=True)

        @block.vector
        def _(dve):
            own = Steps(dve, dve_step)
            V = nc.vector

            def max_of(j):
                a, b = (j, j + 1) if j < JOBS - 1 else (JOBS - 1, MAXES)
                dve.wait_ge(stage_in[j % 2], 16 * (j // 2 + 1))
                src = stage[:, j % 2, 0:(b - a) * 512].rearrange("p (n w) -> p n w", n=b - a) if b - a > 1 \
                    else stage[:, j % 2, :]
                V.tensor_reduce(pmax[:, a:b], src, AX_X, ALU.max, apply_absolute_value=True)\
                    .then_inc(pmax_ready, 1)

            def scale(j):
                a, b = (j, j + 1) if j < JOBS - 1 else (JOBS - 1, MAXES)
                exp = W_EXP if j < JOBS - 1 else F_EXP
                dve.wait_ge(gmax_ready, j + 1)
                own.run(V.tensor_scalar(p2[:, a:b], gmax[:, a:b], 1e-30, None, ALU.max))
                bits = p2[:, a:b].bitcast(I32)
                own.run(V.tensor_scalar(bits, bits, 0x7F800000, None, ALU.bitwise_and))
                own.run(V.reciprocal(s_w[:, a:b], p2[:, a:b]))
                own.run(V.tensor_scalar(undo[:, a:b], p2[:, a:b], 2.0 ** -(exp + X_EXP), None, ALU.mult))
                if j == 4:
                    own.run(V.tensor_reduce(amax[:, :], p2[:, 1:5], AX_X, ALU.max))
                    own.run(V.reciprocal(s_y[:, :], amax[:, :]))
                    own.run(V.tensor_scalar(s_y[:, :], s_y[:, :], 2.0 ** Y_EXP, None, ALU.mult))
                if j == 5:
                    own.run(V.scalar_tensor_tensor(undo_out[:, :], amax[:, :], 2.0 ** (-Y_EXP - W_EXP),
                                                   p2[:, 5:6], ALU.mult, ALU.mult))
                if j == 6:
                    own.run(V.tensor_scalar(tanh_in[:, :], undo[:, 6:7], GELU_C, None, ALU.mult))
                    own.run(V.scalar_tensor_tensor(undo_down[:, :], p2[:, 6:7], 2.0 ** (-I_EXP - F_EXP),
                                                   p2[:, 7:8], ALU.mult, ALU.mult))
                    own.run(V.tensor_tensor(undo_down[:, :], undo_down[:, :], p2[:, 8:9], ALU.mult))
                    exp += CODE_EXP
                V.tensor_scalar(s_w[:, a:b], s_w[:, a:b], 2.0 ** exp, None, ALU.mult)\
                    .then_inc(scale_ready, 1)
                dve.wait_ge(scale_ready, j + 1)

            def split_lo(j):
                dve.wait_ge(w_hi_done, j + 1)
                src = stage[:, j % 2, :]
                if j < SECTIONS:
                    hi, lo = (win[:, s, :, j * D:(j + 1) * D] for s in range(2))
                    src = src.rearrange("p (k m) -> p k m", k=KT)
                else:
                    hi, lo = (wout[:, s, :, :].rearrange("p c m -> p (c m)") for s in range(2))
                V.scalar_tensor_tensor(lo, src, s_w[:, j:j + 1], hi, ALU.mult, ALU.subtract)\
                    .then_inc(w_done, 1)

            def norm(n, t, dst=xn):
                for b in range(BLOCKS):
                    own.mark(V.bn_stats(stats[:, b, :], h[:, t * BLOCKS + b, :]))
                own.settle()
                for b in range(BLOCKS):
                    last = V.bn_aggr(mv[:, b, :], stats[:, b, :])
                    if b < BLOCKS - 1:
                        own.mark(last)
                last.then_inc(var_ready, 1)
                dve.wait_ge(std_ready, n + 1)
                own.run(V.reciprocal(rstd[:, :], rstd[:, :]))
                own.run(V.tensor_scalar(rstd[:, :], rstd[:, :], 2.0 ** X_EXP, None, ALU.mult))
                for b in range(BLOCKS):
                    V.tensor_scalar(dst[:, b, :], h[:, t * BLOCKS + b, :], mv[:, b, 0:1], rstd[:, b:b + 1],
                                    ALU.subtract, ALU.mult).then_inc(xn_ready, 1)

            def norm_1_of(t):
                dve.wait_ge(h_copied, BLOCKS * t + BLOCKS)
                own.run(V.memset(stats[:, :, :], 0.0))
                norm(norm_1(t), t)

            def x_lo(n, t, bank=4):
                for k in range(KT):
                    dve.wait_ge(x_hi_done, KT * n + k + 1)
                    V.tensor_tensor(xT[:, 1, k, tile_cols(t)], ps[:, bank + k, :],
                                    xT[:, 0, k, tile_cols(t)], ALU.subtract).then_inc(x_done, 1)

            def y_lo(t, c):
                dve.wait_ge(y_hi_done, CT * t + c + 1)
                V.scalar_tensor_tensor(y_hl[:, 1, c, :], sg[:, c % 2, :], s_y[:, 0:1], y_hl[:, 0, c, :],
                                       ALU.mult, ALU.subtract).then_inc(y_done, 1)

            def unit(t, c):
                u, b = CT * t + c, c % 2
                dve.wait_ge(a_sig, u + 1)
                a, w = sa[:, b, :], tk[:, b, :]
                own.run(V.tensor_scalar(starts[:, ::CHUNK], sa[:, b, ::CHUNK], A_LO, A_HI, ALU.max, ALU.min))
                own.run(V.tensor_scalar(a, a, A_LO, A_HI, ALU.max, ALU.min))
                own.run(V.memset(sa[:, b, ::SEQ_LEN], 0.0))
                own.run(V.tensor_tensor_scan(mem[:, :], a, starts[:, :], 0.0, ALU.mult, ALU.max))
                own.run(V.tensor_scalar(mem[:, :], mem[:, :], 1.0 / PREFIX_LO, 1.0, ALU.mult, ALU.min))
                dve.wait_ge(u_ready, u + 1)
                own.run(V.tensor_tensor(w, mem[:, :], w, ALU.mult))
                own.run(V.tensor_tensor_scan(mem[:, :], a, w, 0.0, ALU.mult, ALU.add))
                if c == 0:
                    for i in range(CT):
                        dve.wait_ge(rinv_spread, CT * t + i + 1)
                        V.tensor_tensor(qs[:, i, :], qs[:, i, :], ps[:, 4 + i, :], ALU.mult)\
                            .then_inc(q_normed, 1)
                    dve.wait_ge(q_normed, CT * t + CT)
                own.run(V.tensor_tensor(mem[:, :], mem[:, :], qs[:, c, :], ALU.mult))
                own.run(V.tensor_tensor(mem[:, :], mem[:, :], vs[:, b, :], ALU.subtract))
                dve.wait_ge(g_sig, u + 1)
                own.run(V.tensor_tensor(sg[:, b, :], sg[:, b, :], mem[:, :], ALU.mult))
                V.tensor_tensor(sg[:, b, :], sg[:, b, :], vs[:, b, :], ALU.add).then_inc(y_ready, 1)

            def dequantise(n, slot, par, m, half, in_slot):
                raw = stage[:, slot, half * 512:(half + 1) * 512].bitcast(I32)
                scl = stage[:, slot, WORDS + half * 512:WORDS + (half + 1) * 512]
                dve.wait_ge(raw_in[slot], 32 * (in_slot + 1))
                own.run(V.scalar_tensor_tensor(raw, raw, 12, raw, ALU.logical_shift_left, ALU.bitwise_or))
                own.run(V.tensor_scalar(mag[:, :], raw, 0x00070007, 9, ALU.bitwise_and,
                                        ALU.logical_shift_left))
                own.run(V.tensor_scalar(raw, raw, 0x00080008, 12, ALU.bitwise_and, ALU.logical_shift_left))
                own.run(V.tensor_tensor(raw, raw, mag[:, :], ALU.bitwise_or))
                val = stage[:, slot, half * 512:(half + 1) * 512].bitcast(F16)
                for i in range(2):
                    k = 4 * n + 2 * half + i
                    if not (isinstance(k, int) and k < 2):
                        dve.wait_ge(f_done, k - 1)
                    if m < 2:
                        v = val[:, 512 * i:512 * (i + 1)].rearrange("p (w k) -> p k w", k=2)
                        s = scl[:, 256 * i:256 * (i + 1)].unsqueeze(1).broadcast_to([P, 2, 256])
                        o = wf[:, i, :].rearrange("p (k w) -> p k w", k=2)
                    else:
                        v = val.rearrange("p (w k) -> p k w", k=2)[:, i, :]
                        s, o = scl, wf[:, i, :]
                    V.scalar_tensor_tensor(o, v, s_ffn[:, m:m + 1], s, ALU.mult, ALU.mult)\
                        .then_inc(wf_ready, 1)

            def attention(t, first=False, last=False):
                dve.wait_ge(sum_rooted, t + 1)
                V.reciprocal(rinv[:, :], rinv[:, :]).then_inc(rinv_ready, 1)
                unit(t, 0)
                if first:
                    max_of(4)
                    scale(4)
                    split_lo(4)
                unit(t, 1)
                y_lo(t, 0)
                if first:
                    max_of(5)
                    scale(5)
                    split_lo(5)
                else:
                    x_lo(norm_2(t - 1), t - 1)
                if last:
                    dequantise(0, 0, 0, 0, 0, 0)
                    dequantise(0, 0, 0, 0, 1, 0)
                else:
                    norm_1_of(t + 1)
                unit(t, 2)
                y_lo(t, 1)
                if last:
                    dequantise(1, 1, 0, 1, 0, 0)
                    dequantise(1, 1, 0, 1, 1, 0)
                else:
                    x_lo(norm_1(t + 1), t + 1)
                if first:
                    max_of(6)
                    scale(6)
                unit(t, 3)
                y_lo(t, 2)
                y_lo(t, 3)
                if last:
                    dequantise(2, 0, 0, 2, 0, 1)
                    dequantise(2, 0, 0, 2, 1, 1)
                for b in range(BLOCKS):
                    dve.wait_ge(attn_out, BLOCKS * t + b + 1)
                    blk = h[:, t * BLOCKS + b, :]
                    V.scalar_tensor_tensor(blk, ps[:, b, :], undo_out[:, 0:1], blk, ALU.mult, ALU.add)\
                        .then_inc(attn_added, 1)
                dve.wait_ge(attn_added, BLOCKS * t + BLOCKS)
                own.run(V.memset(stats[:, :, :], 0.0))
                norm(norm_2(t), t, xn_last if last else xn)
                if last:
                    x_lo(norm_2(t), t, 0)
                own.restart()

            def add_down(tile_index, t):
                for b in range(BLOCKS):
                    dve.wait_ge(down_made, BLOCKS * tile_index + b + 1)
                    blk = h[:, t * BLOCKS + b, :]
                    V.scalar_tensor_tensor(blk, ps[:, b, :], undo_down[:, 0:1], blk, ALU.mult, ALU.add)\
                        .then_inc(down_added, 1)

            def ffn_group(group, par, pair, last=False, first=False):
                for s in range(STEPS):
                    index, b = STEPS * group + s, s % 2
                    gate, up = ps[:, 4 + 2 * b, :], ps[:, 5 + 2 * b, :]
                    dve.wait_ge(gate_squared, index + 1)
                    own.run(V.tensor_scalar(sq[:, b, :], sq[:, b, :], GELU_A, 1.0, ALU.mult, ALU.add))
                    V.tensor_tensor(sq[:, b, :], sq[:, b, :], gate, ALU.mult).then_inc(inner_ready, 1)
                    if s >= 2 and s % 2 == 0 and s <= 12 and not last:
                        piece = (s - 2) // 2
                        m, half = piece // 2, piece % 2
                        n = 6 * pair + 3 * (par + 1) + m
                        dequantise(n, (par + 1 + m) % 2, 1 - par, m, half,
                                   3 * pair + (3 * (par + 1) + m) // 2)
                    dve.wait_ge(tanh_done, index + 1)
                    own.run(V.scalar_tensor_tensor(th[:, b, :], th[:, b, :], 1.0, gate, ALU.add, ALU.mult))
                    dve.wait_ge(up_made, index + 1)
                    V.scalar_tensor_tensor(th[:, b, :], th[:, b, :],
                                           0.5 * 2.0 ** (I_EXP - 2 * (F_EXP + X_EXP)), up,
                                           ALU.mult, ALU.mult).then_inc(inter_ready, 1)
                    dve.wait_ge(inter_hi, index + 1)
                    V.tensor_tensor(inter[:, b, 1, :], th[:, b, :], inter[:, b, 0, :], ALU.subtract)\
                        .then_inc(inter_done, 1)
                    if s % GROUP == 0 and not (first and s == 0):
                        add_down(TILES * group + s // GROUP - 1, (s // GROUP - 1) % TILES)
                own.restart()

            s_ffn = s_w[:, 6:9]
            dve.wait_ge(ids_in, 16)
            own.run(V.tensor_scalar(ids_f[:, 0, :], ids_sb[:, :], 0.0, float(VOCAB), ALU.is_lt, ALU.mult))
            own.run(V.tensor_tensor(ids_f[:, 1, :], ids_f[:, 0, :], ids_sb[:, :], ALU.add))
            V.tensor_scalar(rows[:, :], ids_f[:, 1, :], 0.0, float(VOCAB - 1), ALU.max, ALU.min)\
                .then_inc(rows_ready, 1)
            own.mark(V.memset(starts[:, :], 0.0))
            max_of(0)
            max_of(1)
            scale(0)
            split_lo(0)
            dve.wait_ge(h_copied, BLOCKS)
            norm(0, 0)
            scale(1)
            split_lo(1)
            x_lo(0, 0)
            for j in (2, 3):
                max_of(j)
                scale(j)
                split_lo(j)
            own.restart()
            attention(0, first=True)
            with dve.Fori(1, TILES - 1) as t:
                attention(t)
            attention(TILES - 1, last=True)
            ffn_group(0, 0, 0, first=True)
            ffn_group(1, 1, 0)
            with dve.Fori(1, PAIRS - 1) as pair:
                ffn_group(2 * pair, 0, pair)
                ffn_group(2 * pair + 1, 1, pair)
            ffn_group(GROUPS - 2, 0, PAIRS - 1)
            ffn_group(GROUPS - 1, 1, PAIRS - 1, last=True)
            add_down(TILES * GROUPS - 1, TILES - 1)


def kernel(x, L0_tok_E, L0_tok_P, L0_attn_w_in, L0_attn_w_out, L0_ffn_gate_W_packed, L0_ffn_gate_scales,
           L0_ffn_up_W_packed, L0_ffn_up_scales, L0_ffn_down_W_packed, L0_ffn_down_scales):
    import numpy as np
    import concourse.bacc as bacc
    from concourse.bass_utils import run_bass_kernel_spmd

    def array(a):
        return np.asarray(a)

    def rows_by_channel(w):
        m = w.shape[0]
        return w.reshape(m, 2, P, 2).transpose(2, 3, 1, 0).reshape(P, KT, m)

    def up_words(w):
        return w.reshape(GROUPS, 2, P, 2, 2, P).transpose(0, 5, 1, 3, 4, 2).reshape(GROUPS, P, WORDS)

    def up_scales(w):
        return w.reshape(GROUPS, 2, P, 2, 2, 8).transpose(0, 5, 1, 3, 4, 2).reshape(GROUPS, 8, WORDS)

    def down_words(w):
        return w.reshape(D, GROUPS, 2, P).transpose(1, 3, 2, 0).reshape(GROUPS, P, WORDS)

    def down_scales(w):
        return w.reshape(D, GROUPS, 2, 8).transpose(1, 3, 2, 0).reshape(GROUPS, 8, WORDS)

    gate_s, up_s, down_s = (array(a) for a in (L0_ffn_gate_scales, L0_ffn_up_scales, L0_ffn_down_scales))
    w_in = rows_by_channel(array(L0_attn_w_in))
    arrays = {
        "ids": array(x).T,
        "table": array(L0_tok_E),
        "p_t": array(L0_tok_P).T,
        "w_in": np.concatenate([w_in[None, :, :, 0:D], w_in[:, :, D:].reshape(P, KT, 4, CT, P)
                                .transpose(3, 0, 1, 2, 4).reshape(CT, P, KT, D)]).reshape(1 + CT, P, KT * D),
        "w_out": array(L0_attn_w_out).T.reshape(CT, P, D).transpose(1, 0, 2).reshape(P, CT * D),
        "all_scales": np.concatenate([a.reshape(P, 512) for a in (gate_s, up_s, down_s)], axis=1),
        "packed": np.stack([up_words(array(L0_ffn_gate_W_packed)), up_words(array(L0_ffn_up_W_packed)),
                            down_words(array(L0_ffn_down_W_packed))], axis=1).reshape(3 * GROUPS, P, WORDS),
        "scales": np.stack([up_scales(gate_s), up_scales(up_s), down_scales(down_s)],
                           axis=1).reshape(3 * GROUPS, 8, WORDS),
    }
    arrays = {k: np.ascontiguousarray(v) for k, v in arrays.items()}
    nc = bacc.Bacc("TRN2", target_bir_lowering=False, num_devices=1)
    aps = [nc.dram_tensor(k, v.shape, mybir.dt.from_np(v.dtype), kind="ExternalInput").ap()
           for k, v in arrays.items()]
    out = nc.dram_tensor("out", (SEQS, SEQ_LEN, D), F32, kind="ExternalOutput").ap()
    lm_layer(nc, *aps, out.rearrange("s p d -> p s d"))
    result = run_bass_kernel_spmd(nc, [arrays], core_ids=[0])
    return result.results[0]["out"]
```

```python
from contextlib import ExitStack

import concourse.bass as bass
from concourse import mybir

F32 = mybir.dt.float32
F16 = mybir.dt.float16
BF16 = mybir.dt.bfloat16
I32 = mybir.dt.int32
U32 = mybir.dt.uint32
ALU = mybir.AluOpType
ACT = mybir.ActivationFunctionType
AX_X = mybir.AxisListType.X

P = 128
SEQS, SEQ_LEN = 16, 128
VOCAB, D_EMBED, D = 32000, 128, 512
MLP = 4096
HEAD_DIM, CHUNK = 32, 64
TOKENS = SEQS * SEQ_LEN
TILE = 512
TILES = TOKENS // TILE
BLOCKS = TILE // P
KT = D // P
CT = D // P
SECTIONS = 5
SUM_ROWS = 3 * 32
RMS_EPS, LN_EPS = 1.1920928955078125e-07, 1e-05
A_LO, A_HI, PREFIX_LO = 0.6, 0.9995, 1e-06
GROUP = 4
GROUPS = MLP // (GROUP * P)
PAIRS = GROUPS // 2
STEPS = TILES * GROUP
WORDS = 1024

W_EXP = 14
F_EXP = 12
CODE_EXP = 14
X_EXP = 11
Y_EXP = -5
I_EXP = -11
GELU_A, GELU_C = 0.044715, 0.7978845608028654

WARM = (34, 10, 6)
JOBS = 7
DVE_JOBS = 4
MAXES = 9


class Steps:

    def __init__(self, eng, sem):
        self.eng, self.sem, self.n = eng, sem, 0

    def mark(self, instruction):
        instruction.then_inc(self.sem, 1)
        self.n += 1

    def settle(self):
        self.eng.wait_ge(self.sem, self.n)

    def run(self, instruction):
        self.mark(instruction)
        self.settle()

    def restart(self):
        self.settle()
        self.eng.sem_clear(self.sem)
        self.n = 0


def lm_layer(nc, ids, table, p_t, w_in, w_out, all_scales, packed, scales, out):
    with ExitStack() as ctx:
        def sb(name, shape, dt):
            return ctx.enter_context(nc.sbuf_tensor(name, shape, dt))

        def sem(name):
            return ctx.enter_context(nc.semaphore(name))

        h = sb("h", [P, SEQS, D], F32)
        xT = sb("xT", [P, 2, KT, TOKENS], F16)
        region = sb("region", [P, 10240], F32)
        win = region[:, :].bitcast(F16).rearrange("p (s k m) -> p s k m", s=2, k=KT)
        wout = sb("wout", [P, 2, CT, D], F16)
        even_w = sb("even_w", [P, 3, 2, GROUP, D], F16)
        odd_w = region[:, 0:6144].bitcast(F16).rearrange("p (m s n w) -> p m s n w", s=2, m=3, n=GROUP)
        ffn_w = [even_w, odd_w]
        sq = region[:, 6144:7168].rearrange("p (b t) -> p b t", b=2)
        th = region[:, 7168:8192].rearrange("p (b t) -> p b t", b=2)
        inter = region[:, 8192:9216].bitcast(F16).rearrange("p (b s t) -> p b s t", b=2, s=2)
        stage = sb("stage", [P, 2, 2048], F32)
        tk = sb("tk", [P, 2, TILE], F32)
        vs = sb("vs", [P, 2, TILE], F32)
        sa = sb("sa", [P, 2, TILE], F32)
        sg = sb("sg", [P, 2, TILE], F32)
        mem = sb("mem", [P, TILE], F32)
        starts = sb("starts", [P, TILE], F32)
        qs = sb("qs", [P, CT, TILE], F32)
        q2 = sb("q2", [P, 2, TILE], F32)
        yx = sb("yx", [P, 4 * TILE], F32)
        y_hl = yx[:, :].bitcast(F16).rearrange("p (s c t) -> p s c t", s=2, c=CT)
        xn_last = yx[:, :].rearrange("p (b d) -> p b d", b=BLOCKS)
        emb_area = even_w[:, 1, :, :, :].rearrange("p s n w -> p (s n w)").bitcast(F32)
        emb = emb_area[:, 0:1024].rearrange("p (b s e) -> p b s e", b=2, s=BLOCKS)
        emb_t, pt_sb = emb_area[:, 1024:1536], emb_area[:, 1536:2048]
        xn = even_w[:, 2, :, :, :].rearrange("p s n w -> p (s n w)").bitcast(F32)\
            .rearrange("p (b d) -> p b d", b=BLOCKS)
        rinv = sb("rinv", [SUM_ROWS, TILE], F32)
        rinv_parts = sb("rinv_parts", [SUM_ROWS, TILE], BF16)
        mag = sb("mag", [P, 512], I32)
        wf = sb("wf", [P, 2, 512], F32)
        ident = sb("ident", [P, P], F32)
        head_sum = sb("head_sum", [P, CT, SUM_ROWS], F32)
        head_spread = sb("head_spread", [SUM_ROWS, CT, P], BF16)
        bias = sb("bias", [P, 3], F32)
        warm = sb("warm", [P, 1], F32)
        ids_sb = sb("ids_sb", [P, SEQS], I32)
        ids_f = sb("ids_f", [P, 2, SEQS], F32)
        rows = sb("rows", [P, SEQS], I32)
        pmax = sb("pmax", [P, MAXES], F32)
        gmax = sb("gmax", [P, MAXES], F32)
        amax = sb("amax", [P, 1], F32)
        p2 = sb("p2", [P, MAXES], F32)
        s_w = sb("s_w", [P, MAXES], F32)
        undo = sb("undo", [P, MAXES], F32)
        s_y = sb("s_y", [P, 1], F32)
        undo_out = sb("undo_out", [P, 1], F32)
        undo_down = sb("undo_down", [P, 1], F32)
        tanh_in = sb("tanh_in", [P, 1], F32)
        stats = sb("stats", [P, BLOCKS, 6], F32)
        mv = sb("mv", [P, BLOCKS, 2], F32)
        rstd = sb("rstd", [P, BLOCKS], F32)
        ps = ctx.enter_context(nc.psum_tensor("ps", [P, 8, TILE], F32))

        ids_in, pt_in, out_stored = sem("ids_in"), sem("pt_in"), sem("out_stored")
        emb_in = [sem(f"emb_in{t}") for t in range(TILES)]
        stage_in = [sem(f"stage_in{s}") for s in range(2)]
        raw_in = [sem(f"raw_in{s}") for s in range(2)]
        consts_ready, rows_ready, masks_turned, spread_ready = (
            sem("consts_ready"), sem("rows_ready"), sem("masks_turned"), sem("spread_ready"))
        pmax_ready, gmax_ready = sem("pmax_ready"), sem("gmax_ready")
        scale_ready, w_scaled, w_hi_done, w_done = (
            sem("scale_ready"), sem("w_scaled"), sem("w_hi_done"), sem("w_done"))
        emb_turned, emb_copied, h_made, h_copied = (
            sem("emb_turned"), sem("emb_copied"), sem("h_made"), sem("h_copied"))
        var_ready, std_ready, sum_rooted = sem("var_ready"), sem("std_ready"), sem("sum_rooted")
        xn_ready, x_turned, x_hi_done, x_done = (
            sem("xn_ready"), sem("x_turned"), sem("x_hi_done"), sem("x_done"))
        q_made, q_copied, q_squared, sum_made, rinv_ready, rinv_spread, q_normed = (
            sem("q_made"), sem("q_copied"), sem("q_squared"), sem("sum_made"), sem("rinv_ready"),
            sem("rinv_spread"), sem("q_normed"))
        k_made, v_made, a_made, g_made = sem("k_made"), sem("v_made"), sem("a_made"), sem("g_made")
        k_tanh, v_copied, u_ready, a_sig, g_sig = (
            sem("k_tanh"), sem("v_copied"), sem("u_ready"), sem("a_sig"), sem("g_sig"))
        y_ready, y_hi_done, y_done = sem("y_ready"), sem("y_hi_done"), sem("y_done")
        attn_out, attn_added = sem("attn_out"), sem("attn_added")
        wf_ready, f_hi_done, f_done = sem("wf_ready"), sem("f_hi_done"), sem("f_done")
        gate_made, up_made, gate_squared, inner_ready, tanh_done, inter_ready, inter_hi, inter_done = (
            sem("gate_made"), sem("up_made"), sem("gate_squared"), sem("inner_ready"), sem("tanh_done"),
            sem("inter_ready"), sem("inter_hi"), sem("inter_done"))
        down_made, down_added = sem("down_made"), sem("down_added")
        dve_step, pool_step = sem("dve_step"), sem("pool_step")
        zeros_ready = sem("zeros_ready")

        block = ctx.enter_context(nc.Block())

        def tile_cols(t):
            return bass.ts(t, TILE)

        def norm_1(t):
            return max(0, 2 * t - 1)

        def norm_2(t):
            return 2 * t + 2 if t < TILES - 1 else 2 * TILES - 1

        group_0_pieces = {(1, 0): [(0, 0)], (1, 2): [(0, 1)], (2, 2): [(1, 0)], (2, 3): [(1, 1)],
                          (3, 0): [(2, 0)], (3, 1): [(2, 1)]}

        @block.sync
        def _(sp):
            sp.dma_start(ids_sb[:, :], ids).then_inc(ids_in, 16)
            sp.dma_start(pt_sb, p_t).then_inc(pt_in, 16)
            for j in range(JOBS):
                if j >= 2:
                    sp.wait_ge(w_done, j - 1)
                if j < SECTIONS:
                    src, dst = w_in[j], stage[:, j % 2, :]
                elif j == SECTIONS:
                    src, dst = w_out, stage[:, j % 2, :]
                else:
                    src, dst = all_scales, stage[:, j % 2, 0:1536]
                sp.dma_start(dst, src).then_inc(stage_in[j % 2], 16)

            def load_packed(n, slot):
                sp.dma_start(stage[:, slot, 0:WORDS].bitcast(I32), packed[n]).then_inc(raw_in[slot], 16)
                sp.dma_start(stage[:, slot, WORDS:], scales[n].unsqueeze(1).broadcast_to([8, 16, WORDS]))\
                  .then_inc(raw_in[slot], 16)

            sp.wait_ge(pmax_ready, JOBS)
            load_packed(0, 0)
            sp.wait_ge(w_done, JOBS - 1)
            load_packed(1, 1)

            def later_loads(pair, count):
                for i in range(count):
                    n = 6 * pair + i + 2
                    sp.wait_ge(wf_ready, 4 * (6 * pair + i + 1))
                    load_packed(n, i % 2)

            with sp.Fori(0, PAIRS - 1) as pair:
                later_loads(pair, 6)
            later_loads(PAIRS - 1, 4)
            stores = [(t * BLOCKS, BLOCKS) for t in range(TILES - 1)] + \
                     [((TILES - 1) * BLOCKS + b, 1) for b in range(BLOCKS)]
            for start, count in stores:
                sp.wait_ge(down_added, SEQS * (GROUPS - 1) + start + count)
                sp.dma_start(out[:, start:start + count, :], h[:, start:start + count, :])\
                  .then_inc(out_stored, 16)
            sp.wait_ge(out_stored, 16 * len(stores))

        @block.gpsimd
        def _(pool):
            own = Steps(pool, pool_step)

            def gather(t):
                if t >= 2:
                    pool.wait_ge(emb_turned, t - 1)
                for s in range(BLOCKS):
                    q = BLOCKS * t + s
                    nc.gpsimd.indirect_dma_start(
                        out=emb[:, t % 2, s, :], out_offset=None, in_=table,
                        in_offset=bass.IndirectOffsetOnAxis(ap=rows[:, q:q + 1].bitcast(U32), axis=0),
                    ).then_inc(emb_in[t], 16)

            def max_over_partitions(j):
                a, b = (j, j + 1) if j < JOBS - 1 else (JOBS - 1, MAXES)
                pool.wait_ge(pmax_ready, j + 1)
                nc.gpsimd.partition_all_reduce(gmax[:, a:b], pmax[:, a:b], P,
                                               bass.bass_isa.ReduceOp.max).then_inc(gmax_ready, 1)

            def make_u(t, c):
                u, b = CT * t + c, c % 2
                pool.wait_ge(k_tanh, u + 1)
                pool.wait_ge(v_copied, u + 1)
                nc.gpsimd.tensor_tensor(tk[:, b, :], tk[:, b, :], vs[:, b, :], ALU.mult)\
                    .then_inc(u_ready, 1)

            pool.wait_ge(rows_ready, 1)
            gather(0)
            own.mark(nc.gpsimd.memset(ident[:, :], 0.0))
            own.mark(nc.gpsimd.memset(head_sum[:, :, :], 1.0))
            own.mark(nc.gpsimd.memset(bias[:, 0:1], 2.0))
            own.mark(nc.gpsimd.memset(bias[:, 1:2], RMS_EPS))
            own.mark(nc.gpsimd.memset(bias[:, 2:3], LN_EPS))
            own.settle()
            nc.gpsimd.affine_select(out=ident[:, :], in_=ident[:, :], compare_op=ALU.not_equal,
                                    fill=1.0, base=0, pattern=[[-1, P]], channel_multiplier=1)\
                .then_inc(consts_ready, 1)
            max_over_partitions(0)
            max_over_partitions(1)
            hs = head_sum[:, :, :].rearrange("p c (r h) -> p c r h", r=3)
            own.run(nc.gpsimd.affine_select(out=hs, in_=hs, compare_op=ALU.is_ge, fill=0.0, base=0,
                                            pattern=[[P, CT], [0, 3], [-HEAD_DIM, 32]],
                                            channel_multiplier=1))
            nc.gpsimd.affine_select(out=hs, in_=hs, compare_op=ALU.is_ge, fill=0.0,
                                    base=HEAD_DIM - 1, pattern=[[-P, CT], [0, 3], [HEAD_DIM, 32]],
                                    channel_multiplier=-1).then_inc(consts_ready, 1)
            gather(1)

            def split_lo(j):
                pool.wait_ge(w_hi_done, j + 1)
                src = stage[:, j % 2, :]
                if j < SECTIONS:
                    hi, lo = (win[:, s, :, j * D:(j + 1) * D] for s in range(2))
                    src = src.rearrange("p (k m) -> p k m", k=KT)
                else:
                    hi, lo = (wout[:, s, :, :].rearrange("p c m -> p (c m)") for s in range(2))
                nc.gpsimd.tensor_tensor(lo, src, hi, ALU.subtract).then_inc(w_done, 1)

            def f_lo(n, par, m, half):
                for i in range(2):
                    k = 4 * n + 2 * half + i
                    pool.wait_ge(f_hi_done, k + 1)
                    nc.gpsimd.tensor_tensor(ffn_w[par][:, m, 1, 2 * half + i, :], wf[:, i, :],
                                            ffn_w[par][:, m, 0, 2 * half + i, :],
                                            ALU.subtract).then_inc(f_done, 1)

            def group_lo(n0, par):
                for m in range(3):
                    for half in range(2):
                        f_lo(n0 + m, par, m, half)

            gather(2)
            max_over_partitions(2)
            max_over_partitions(3)
            max_over_partitions(4)
            for t in range(TILES):
                for c in range(CT):
                    make_u(t, c)
                    if t == 0 and c == 0:
                        split_lo(4)
                    if t == 0 and c == 1:
                        max_over_partitions(5)
                        split_lo(5)
                    if t == 0 and c == 3:
                        max_over_partitions(6)
                        gather(3)
                    for m, half in group_0_pieces.get((t, c), ()):
                        f_lo(m, 0, m, half)
            group_lo(3, 1)
            with pool.Fori(1, PAIRS) as pair:
                group_lo(6 * pair, 0)
                group_lo(6 * pair + 3, 1)

        @block.scalar
        def _(act):
            def split_hi(j):
                act.wait_ge(scale_ready, j + 1)
                src, factor = stage[:, j % 2, :], s_w[:, j:j + 1]
                if j >= DVE_JOBS:
                    nc.scalar.activation(src, src, ACT.Identity, scale=factor).then_inc(w_scaled, 1)
                    act.wait_ge(w_scaled, j - DVE_JOBS + 1)
                    factor = 1.0
                if j < SECTIONS:
                    dst = win[:, 0, :, j * D:(j + 1) * D]
                    src = src.rearrange("p (k m) -> p k m", k=KT)
                else:
                    dst = wout[:, 0, :, :].rearrange("p c m -> p (c m)")
                nc.scalar.activation(dst, src, ACT.Identity, scale=factor).then_inc(w_hi_done, 1)

            def deviation(n):
                act.wait_ge(var_ready, n + 1)
                nc.scalar.activation(rstd[:, :], mv[:, :, 1], ACT.Sqrt, bias=bias[:, 2:3])\
                    .then_inc(std_ready, 1)

            def root_sums(t):
                act.wait_ge(sum_made, CT * t + CT)
                nc.scalar.activation(rinv[:, :], ps[0:SUM_ROWS, 4, :], ACT.Sqrt,
                                     bias=bias[0:SUM_ROWS, 1:2], scale=1.0 / HEAD_DIM)\
                    .then_inc(sum_rooted, 1)

            def x_hi(n, t, bank=4):
                for k in range(KT):
                    act.wait_ge(x_turned, KT * n + k + 1)
                    nc.scalar.activation(xT[:, 0, k, tile_cols(t)], ps[:, bank + k, :], ACT.Copy)\
                        .then_inc(x_hi_done, 1)

            def copy_emb(t):
                act.wait_ge(emb_turned, t + 1)
                nc.scalar.activation(emb_t, ps[:, 4, :], ACT.Copy).then_inc(emb_copied, 1)

            def copy_h(t):
                for b in range(BLOCKS):
                    act.wait_ge(h_made, BLOCKS * t + b + 1)
                    nc.scalar.activation(h[:, BLOCKS * t + b, :], ps[:, (5, 6, 7, 4)[b], :], ACT.Copy)\
                        .then_inc(h_copied, 1)

            def copy_q(t, c):
                act.wait_ge(q_made, CT * t + c + 1)
                nc.scalar.activation(qs[:, c, :], ps[:, 4 + c, :], ACT.Identity, scale=undo[:, 0:1])\
                    .then_inc(q_copied, 1)

            def square_q(t, c):
                act.wait_ge(q_copied, CT * t + c + 1)
                if c >= 2:
                    act.wait_ge(sum_made, CT * t + c - 1)
                nc.scalar.activation(q2[:, c % 2, :], qs[:, c, :], ACT.Square).then_inc(q_squared, 1)

            def unit(t, c, after_k=(), after_v=(), after_a=()):
                u, b, col = CT * t + c, c % 2, slice(1 + c, 2 + c)
                if u >= 2:
                    act.wait_ge(y_ready, u - 1)
                act.wait_ge(k_made, u + 1)
                nc.scalar.activation(tk[:, b, :], ps[:, 0, :], ACT.Tanh, scale=undo[:, col])\
                    .then_inc(k_tanh, 1)
                for step in after_k:
                    step()
                act.wait_ge(v_made, u + 1)
                nc.scalar.activation(vs[:, b, :], ps[:, 1, :], ACT.Identity, scale=undo[:, col])\
                    .then_inc(v_copied, 1)
                for step in after_v:
                    step()
                act.wait_ge(a_made, u + 1)
                nc.scalar.activation(sa[:, b, :], ps[:, 2, :], ACT.Sigmoid, bias=bias[:, 0:1],
                                     scale=undo[:, col]).then_inc(a_sig, 1)
                for step in after_a:
                    step()
                if u >= 2:
                    act.wait_ge(y_done, u - 1)
                act.wait_ge(g_made, u + 1)
                nc.scalar.activation(sg[:, b, :], ps[:, 3, :], ACT.Sigmoid, scale=undo[:, col])\
                    .then_inc(g_sig, 1)

            def y_hi(t, c):
                act.wait_ge(y_ready, CT * t + c + 1)
                nc.scalar.activation(y_hl[:, 0, c, :], sg[:, c % 2, :], ACT.Identity, scale=s_y[:, 0:1])\
                    .then_inc(y_hi_done, 1)

            def f_hi(n, par, m, half):
                for i in range(2):
                    act.wait_ge(wf_ready, 4 * n + 2 * half + i + 1)
                    nc.scalar.activation(ffn_w[par][:, m, 0, 2 * half + i, :], wf[:, i, :], ACT.Copy)\
                        .then_inc(f_hi_done, 1)

            def group_0_hi(t, c):
                for m, half in group_0_pieces.get((t, c), ()):
                    f_hi(m, 0, m, half)

            def attention(t):
                first, last = t == 0, t == TILES - 1
                if first:
                    unit(0, 0, after_k=[lambda: split_hi(3)])
                else:
                    unit(t, 0, after_a=[lambda: x_hi(norm_2(t - 1), t - 1)])
                    group_0_hi(t, 0)
                if last:
                    unit(t, 1)
                else:
                    unit(t, 1, after_k=[lambda: copy_emb(t + 1)] + ([lambda: split_hi(4)] if first else []),
                         after_v=[lambda: copy_h(t + 1)],
                         after_a=[lambda: deviation(norm_1(t + 1))])
                y_hi(t, 0)
                if first:
                    split_hi(5)
                group_0_hi(t, 1)
                if last:
                    unit(t, 2, after_v=[lambda: y_hi(t, 1)])
                else:
                    unit(t, 2, after_v=[lambda: x_hi(norm_1(t + 1), t + 1), lambda: y_hi(t, 1)])
                group_0_hi(t, 2)
                unit(t, 3)
                if last:
                    y_hi(t, 2)
                    y_hi(t, 3)
                    return
                for c in range(CT):
                    if c == CT - 1:
                        y_hi(t, 3)
                    copy_q(t + 1, c)
                    square_q(t + 1, c)
                    if c == 0:
                        y_hi(t, 2)
                root_sums(t + 1)
                deviation(norm_2(t))
                group_0_hi(t, 3)

            def ffn_step(s, index):
                b = s % 2
                act.wait_ge(gate_made, index + 1)
                nc.scalar.activation(sq[:, b, :], ps[:, 4 + 2 * b, :], ACT.Square, scale=undo[:, 6:7])\
                    .then_inc(gate_squared, 1)
                act.wait_ge(inner_ready, index + 1)
                nc.scalar.activation(th[:, b, :], sq[:, b, :], ACT.Tanh, scale=tanh_in[:, 0:1])\
                    .then_inc(tanh_done, 1)

            def inter_high(s, index):
                act.wait_ge(inter_ready, index + 1)
                nc.scalar.activation(inter[:, s % 2, 0, :], th[:, s % 2, :], ACT.Copy).then_inc(inter_hi, 1)

            def ffn_group(group, par, first=False, last=False):
                for s in range(2 if first else 0, STEPS):
                    index = STEPS * group + s
                    ffn_step(s, index)
                    if s % 2 == 1 and 3 <= s < 15 and not last:
                        piece = (s - 3) // 2
                        f_hi(3 * (group + 1) + piece // 2, 1 - par, piece // 2, piece % 2)
                    inter_high(s, index)
                    if first and s == 2:
                        deviation(norm_2(TILES - 1))
                    if first and s == GROUP:
                        x_hi(norm_2(TILES - 1), TILES - 1, 0)

            act.wait_ge(consts_ready, 1)
            nc.scalar.activation(warm[:, :], bias[:, 0:1], ACT.Sqrt)
            copy_emb(0)
            copy_h(0)
            deviation(0)
            act.wait_ge(masks_turned, 1)
            nc.scalar.activation(head_spread[:, :, :].rearrange("p c m -> p (c m)"), ps[0:SUM_ROWS, 0, :],
                                 ACT.Copy).then_inc(spread_ready, 1)
            split_hi(0)
            x_hi(0, 0, 0)
            split_hi(1)
            for c in range(2):
                copy_q(0, c)
                square_q(0, c)
            copy_q(0, 2)
            copy_q(0, 3)
            square_q(0, 2)
            square_q(0, 3)
            root_sums(0)
            split_hi(2)
            for t in range(TILES):
                attention(t)
            act.wait_ge(scale_ready, JOBS)
            for s in range(2):
                ffn_step(s, s)
                inter_high(s, s)
            ffn_group(0, 0, first=True)
            ffn_group(1, 1)
            with act.Fori(1, PAIRS - 1) as pair:
                ffn_group(2 * pair, 0)
                ffn_group(2 * pair + 1, 1)
            ffn_group(GROUPS - 2, 0)
            ffn_group(GROUPS - 1, 1, last=True)

        @block.tensor
        def _(pe):
            def products(dst, terms, sem_done=None, n=1):
                for i, (w, x) in enumerate(terms):
                    last = nc.tensor.matmul(dst, w, x, start=(i == 0), stop=(i == len(terms) - 1))
                if sem_done is not None:
                    last.then_inc(sem_done, n)

            def in_terms(sec, c, t):
                at = c * P if sec == 0 else (1 + c) * D + (sec - 1) * P
                cols = slice(at, at + P)
                return [(win[:, a, k, cols], xT[:, b, k, tile_cols(t)])
                        for k in range(KT) for a, b in ((0, 0), (0, 1), (1, 0))]

            def turn_tokens(n, src_of=xn, bank=4, q_left=None):
                pe.wait_ge(xn_ready, BLOCKS * n + BLOCKS)
                for k in range(KT):
                    if q_left is not None:
                        pe.wait_ge(q_normed, q_left + k + 1)
                    nib, half = k // 2, k % 2
                    for b in range(BLOCKS):
                        src = src_of[:, b, 256 * half:256 * half + 256].rearrange("p (m i) -> p i m", i=2)
                        last = nc.tensor.transpose(ps[:, bank + k, b * P:(b + 1) * P], src[:, nib, :],
                                                   ident[:, :])
                    last.then_inc(x_turned, 1)

            def turn_emb(t, b_of):
                for b in range(BLOCKS):
                    last = nc.tensor.transpose(ps[:, 4, b * P:(b + 1) * P], emb[:, b_of, b, :], ident[:, :])
                last.then_inc(emb_turned, 1)

            def make_h(t):
                pe.wait_ge(emb_copied, t + 1)
                for b in range(BLOCKS):
                    nc.tensor.matmul(ps[:, (5, 6, 7, 4)[b], :], emb_t[:, b * P:(b + 1) * P], pt_sb,
                                     start=True, stop=True).then_inc(h_made, 1)

            def make_q(t, c):
                products(ps[:, 4 + c, :], in_terms(0, c, t), q_made)

            def sum_squares(t, c):
                pe.wait_ge(q_squared, CT * t + c + 1)
                nc.tensor.matmul(ps[0:SUM_ROWS, 4, :], head_sum[:, c, :], q2[:, c % 2, :], start=(c == 0),
                                 stop=(c == CT - 1)).then_inc(sum_made, 1)

            def spread_rinv(t):
                pe.wait_ge(q_copied, CT * t + CT)
                pe.wait_ge(rinv_ready, t + 1)
                for c in range(CT):
                    nc.tensor.matmul(ps[:, 4 + c, :], head_spread[:, c, :], rinv_parts[:, :],
                                     start=True, stop=True).then_inc(rinv_spread, 1)

            def unit(t, c, after_k=(), after_v=(), after_a=()):
                u = CT * t + c
                if t == 0:
                    pe.wait_ge(w_done, c + 2)
                for i, (made, read, steps) in enumerate((
                        (k_made, k_tanh, after_k), (v_made, v_copied, after_v), (a_made, a_sig, after_a),
                        (g_made, g_sig, ()))):
                    if u > 0:
                        pe.wait_ge(read, u)
                    if t > 0 and c == 0:
                        pe.wait_ge(attn_added, BLOCKS * (t - 1) + i + 1)
                    products(ps[:, i, :], in_terms(1 + i, c, t), made)
                    for step in steps:
                        step()

            def first_q():
                for i, (w, x) in enumerate(((0, 0), (0, 1), (1, 0))):
                    if i == 0:
                        pe.wait_ge(w_hi_done, 1)
                        pe.wait_ge(x_hi_done, KT)
                    elif i == 1:
                        pe.wait_ge(x_done, KT)
                    else:
                        pe.wait_ge(w_done, 1)
                    for c in range(CT):
                        for k in range(KT):
                            last = nc.tensor.matmul(ps[:, 4 + c, :], win[:, w, k, c * P:(c + 1) * P],
                                                    xT[:, x, k, tile_cols(0)], start=(i == 0 and k == 0),
                                                    stop=(i == 2 and k == KT - 1))
                        if i == 2:
                            last.then_inc(q_made, 1)

            def keep_warm(n, bank):
                zeros = starts[:, :].bitcast(F16)
                for _ in range(n):
                    nc.tensor.matmul(ps[:, bank, :], zeros[:, 0:P], zeros[:, 0:TILE], start=True, stop=True)

            def project(t, b, bank):
                products(ps[:, bank, :],
                         [(y_hl[:, x, c, b * P:(b + 1) * P], wout[:, w, c, :])
                          for c in range(CT) for x, w in ((0, 0), (0, 1), (1, 0))], attn_out)

            def attention(t):
                last = t == TILES - 1

                def next_emb():
                    pe.wait_ge(emb_in[t + 1], 16 * BLOCKS)
                    if t == 0:
                        pe.wait_ge(q_normed, CT)
                    else:
                        pe.wait_ge(x_done, KT * (norm_2(t - 1) + 1))
                    turn_emb(t + 1, (t + 1) % 2)

                def turn_2():
                    turn_tokens(norm_2(t - 1), q_left=CT * t)

                def turn_1():
                    pe.wait_ge(h_copied, BLOCKS * (t + 1) + BLOCKS)
                    turn_tokens(norm_1(t + 1))

                if t == 0:
                    unit(0, 0)
                    spread_rinv(0)
                else:
                    unit(t, 0, after_v=[lambda: spread_rinv(t)], after_a=[turn_2])
                if last:
                    for c in range(1, CT):
                        unit(t, c)
                    pe.wait_ge(x_done, KT * (norm_2(t - 1) + 1))
                    pe.wait_ge(f_done, 8)
                    gate_up(0, 0, 0)
                    gate_up(1, 0, 0)
                else:
                    unit(t, 1, after_k=[next_emb], after_v=[lambda: make_h(t + 1)])
                    unit(t, 2, after_v=[turn_1])
                    unit(t, 3)
                    pe.wait_ge(x_done, KT * (norm_1(t + 1) + 1))
                    make_q(t + 1, 0)
                    for c in range(1, CT):
                        make_q(t + 1, c)
                        sum_squares(t + 1, c - 1)
                for read in (k_tanh, v_copied, a_sig, g_sig):
                    pe.wait_ge(read, CT * t + CT)
                pe.wait_ge(y_done, CT * t + CT)
                for b in range(BLOCKS):
                    project(t, b, b)
                    if b == 0 and not last:
                        sum_squares(t + 1, CT - 1)

            def gate_up(s, par, t):
                ni, b = s % GROUP, s % 2
                for m, made in ((0, gate_made), (1, up_made)):
                    products(ps[:, 4 + 2 * b + m, :],
                             [(ffn_w[par][:, m, w, ni, k * P:(k + 1) * P], xT[:, x, k, tile_cols(t)])
                              for k in range(KT) for w, x in ((0, 0), (0, 1), (1, 0))], made)

            def down(s, par, index, tile_index):
                ni = s % GROUP
                pe.wait_ge(inter_done, index + 1)
                for b in range(BLOCKS):
                    if ni == 0:
                        if isinstance(tile_index, int) and tile_index == 0:
                            pe.wait_ge(attn_added, BLOCKS * (TILES - 1) + b + 1)
                        elif isinstance(tile_index, int) and tile_index == 1:
                            pe.wait_ge(x_done, KT * norm_2(TILES - 1) + b + 1)
                        else:
                            pe.wait_ge(down_added, BLOCKS * tile_index - (BLOCKS - 1 - b))
                    for i, (x, w) in enumerate(((0, 0), (0, 1), (1, 0))):
                        last = nc.tensor.matmul(ps[:, b, :], inter[:, s % 2, x, b * P:(b + 1) * P],
                                                ffn_w[par][:, 2, w, ni, :],
                                                start=(ni == 0 and i == 0), stop=(ni == GROUP - 1 and i == 2))
                    if ni == GROUP - 1:
                        last.then_inc(down_made, 1)

            def ffn_group(group, par, last=False, first=False):
                for s in range(STEPS):
                    if first and s == 0:
                        pe.wait_ge(f_done, 12)
                    elif s + 1 < STEPS:
                        gate_up(s + 1, par, (s + 1) // GROUP)
                    elif not last:
                        pe.wait_ge(f_done, 12 * (group + 2))
                        gate_up(0, 1 - par, 0)
                    if first and s == GROUP:
                        pe.wait_ge(down_added, BLOCKS)
                        turn_tokens(norm_2(TILES - 1), xn_last, 0)
                    down(s, par, STEPS * group + s, TILES * group + s // GROUP)

            pe.wait_ge(zeros_ready, 1)
            keep_warm(WARM[0], 1)
            pe.wait_ge(consts_ready, 1)
            pe.wait_ge(emb_in[0], 16 * BLOCKS)
            turn_emb(0, 0)
            pe.wait_ge(pt_in, 16)
            make_h(0)
            pe.wait_ge(consts_ready, 2)
            for c in range(CT):
                last = nc.tensor.transpose(ps[0:SUM_ROWS, 0, c * P:(c + 1) * P], head_sum[:, c, :],
                                           ident[:, :])
            last.then_inc(masks_turned, 1)
            keep_warm(WARM[1], 1)
            pe.wait_ge(h_copied, BLOCKS)
            pe.wait_ge(spread_ready, 1)
            turn_tokens(0, bank=0)
            keep_warm(WARM[2], 4)
            first_q()
            for c in range(CT):
                sum_squares(0, c)
            for t in range(TILES):
                attention(t)
            ffn_group(0, 0, first=True)
            ffn_group(1, 1)
            with pe.Fori(1, PAIRS - 1) as pair:
                ffn_group(2 * pair, 0)
                ffn_group(2 * pair + 1, 1)
            ffn_group(GROUPS - 2, 0)
            ffn_group(GROUPS - 1, 1, last=True)

        @block.vector
        def _(dve):
            own = Steps(dve, dve_step)
            V = nc.vector

            def max_of(j):
                a, b = (j, j + 1) if j < JOBS - 1 else (JOBS - 1, MAXES)
                dve.wait_ge(stage_in[j % 2], 16 * (j // 2 + 1))
                src = stage[:, j % 2, 0:(b - a) * 512].rearrange("p (n w) -> p n w", n=b - a) if b - a > 1 \
                    else stage[:, j % 2, :]
                V.tensor_reduce(pmax[:, a:b], src, AX_X, ALU.max, apply_absolute_value=True)\
                    .then_inc(pmax_ready, 1)

            def scale(j):
                a, b = (j, j + 1) if j < JOBS - 1 else (JOBS - 1, MAXES)
                exp = W_EXP if j < JOBS - 1 else F_EXP
                dve.wait_ge(gmax_ready, j + 1)
                own.run(V.tensor_scalar(p2[:, a:b], gmax[:, a:b], 1e-30, None, ALU.max))
                bits = p2[:, a:b].bitcast(I32)
                own.run(V.tensor_scalar(bits, bits, 0x7F800000, None, ALU.bitwise_and))
                own.run(V.reciprocal(s_w[:, a:b], p2[:, a:b]))
                own.run(V.tensor_scalar(undo[:, a:b], p2[:, a:b], 2.0 ** -(exp + X_EXP), None, ALU.mult))
                if j == 4:
                    own.run(V.tensor_reduce(amax[:, :], p2[:, 1:5], AX_X, ALU.max))
                    own.run(V.reciprocal(s_y[:, :], amax[:, :]))
                    own.run(V.tensor_scalar(s_y[:, :], s_y[:, :], 2.0 ** Y_EXP, None, ALU.mult))
                if j == 5:
                    own.run(V.scalar_tensor_tensor(undo_out[:, :], amax[:, :], 2.0 ** (-Y_EXP - W_EXP),
                                                   p2[:, 5:6], ALU.mult, ALU.mult))
                if j == 6:
                    own.run(V.tensor_scalar(tanh_in[:, :], undo[:, 6:7], GELU_C, None, ALU.mult))
                    own.run(V.scalar_tensor_tensor(undo_down[:, :], p2[:, 6:7], 2.0 ** (-I_EXP - F_EXP),
                                                   p2[:, 7:8], ALU.mult, ALU.mult))
                    own.run(V.tensor_tensor(undo_down[:, :], undo_down[:, :], p2[:, 8:9], ALU.mult))
                    exp += CODE_EXP
                V.tensor_scalar(s_w[:, a:b], s_w[:, a:b], 2.0 ** exp, None, ALU.mult)\
                    .then_inc(scale_ready, 1)
                dve.wait_ge(scale_ready, j + 1)

            def split_lo(j):
                dve.wait_ge(w_hi_done, j + 1)
                src = stage[:, j % 2, :]
                hi, lo = (win[:, s, :, j * D:(j + 1) * D] for s in range(2))
                src = src.rearrange("p (k m) -> p k m", k=KT)
                V.scalar_tensor_tensor(lo, src, s_w[:, j:j + 1], hi, ALU.mult, ALU.subtract)\
                    .then_inc(w_done, 1)

            def norm_stats(t, b):
                own.mark(V.bn_stats(stats[:, b, :], h[:, t * BLOCKS + b, :]))

            def norm(n, t, dst=xn):
                own.settle()
                for b in range(BLOCKS):
                    last = V.bn_aggr(mv[:, b, :], stats[:, b, :])
                    if b < BLOCKS - 1:
                        own.mark(last)
                last.then_inc(var_ready, 1)
                dve.wait_ge(std_ready, n + 1)
                own.run(V.reciprocal(rstd[:, :], rstd[:, :]))
                own.run(V.tensor_scalar(rstd[:, :], rstd[:, :], 2.0 ** X_EXP, None, ALU.mult))
                for b in range(BLOCKS):
                    V.tensor_scalar(dst[:, b, :], h[:, t * BLOCKS + b, :], mv[:, b, 0:1], rstd[:, b:b + 1],
                                    ALU.subtract, ALU.mult).then_inc(xn_ready, 1)

            def norm_1_of(t):
                for b in range(BLOCKS):
                    dve.wait_ge(h_copied, BLOCKS * t + b + 1)
                    norm_stats(t, b)
                norm(norm_1(t), t)

            def rinv_of(t):
                dve.wait_ge(sum_rooted, t + 1)
                own.mark(V.reciprocal(rinv[:, :], rinv[:, :]))

            def split_rinv():
                own.settle()
                own.run(V.tensor_copy(rinv_parts[:, :], rinv[:, :]))
                own.mark(V.tensor_tensor(rinv_parts[32:64, :], rinv[32:64, :], rinv_parts[32:64, :],
                                         ALU.subtract))
                own.run(V.tensor_tensor(rinv[64:96, :], rinv[64:96, :], rinv_parts[64:96, :],
                                        ALU.subtract))
                own.run(V.tensor_copy(rinv_parts[64:96, :], rinv[64:96, :]))
                V.tensor_tensor(rinv_parts[64:96, :], rinv[64:96, :], rinv_parts[64:96, :],
                                ALU.subtract).then_inc(rinv_ready, 1)

            def norm_q(t):
                for c in range(CT):
                    dve.wait_ge(rinv_spread, CT * t + c + 1)
                    V.tensor_tensor(qs[:, c, :], qs[:, c, :], ps[:, 4 + c, :], ALU.mult)\
                        .then_inc(q_normed, 1)

            def x_lo(n, t, bank=4):
                for k in range(KT):
                    dve.wait_ge(x_hi_done, KT * n + k + 1)
                    V.tensor_tensor(xT[:, 1, k, tile_cols(t)], ps[:, bank + k, :],
                                    xT[:, 0, k, tile_cols(t)], ALU.subtract).then_inc(x_done, 1)

            def y_lo(t, c):
                dve.wait_ge(y_hi_done, CT * t + c + 1)
                V.scalar_tensor_tensor(y_hl[:, 1, c, :], sg[:, c % 2, :], s_y[:, 0:1], y_hl[:, 0, c, :],
                                       ALU.mult, ALU.subtract).then_inc(y_done, 1)

            def unit(t, c):
                u, b = CT * t + c, c % 2
                dve.wait_ge(a_sig, u + 1)
                a, w = sa[:, b, :], tk[:, b, :]
                own.run(V.tensor_scalar(starts[:, ::CHUNK], sa[:, b, ::CHUNK], A_LO, A_HI, ALU.max, ALU.min))
                own.run(V.tensor_scalar(a, a, A_LO, A_HI, ALU.max, ALU.min))
                own.run(V.memset(sa[:, b, ::SEQ_LEN], 0.0))
                own.run(V.tensor_tensor_scan(mem[:, :], a, starts[:, :], 0.0, ALU.mult, ALU.max))
                own.run(V.tensor_scalar(mem[:, :], mem[:, :], 1.0 / PREFIX_LO, 1.0, ALU.mult, ALU.min))
                dve.wait_ge(u_ready, u + 1)
                own.run(V.tensor_tensor(w, mem[:, :], w, ALU.mult))
                own.run(V.tensor_tensor_scan(mem[:, :], a, w, 0.0, ALU.mult, ALU.add))
                dve.wait_ge(q_normed, CT * t + c + 1)
                own.run(V.tensor_tensor(mem[:, :], mem[:, :], qs[:, c, :], ALU.mult))
                own.run(V.tensor_tensor(mem[:, :], mem[:, :], vs[:, b, :], ALU.subtract))
                dve.wait_ge(g_sig, u + 1)
                own.run(V.tensor_tensor(sg[:, b, :], sg[:, b, :], mem[:, :], ALU.mult))
                V.tensor_tensor(sg[:, b, :], sg[:, b, :], vs[:, b, :], ALU.add).then_inc(y_ready, 1)

            def dequantise(n, slot, par, m, half, in_slot):
                raw = stage[:, slot, half * 512:(half + 1) * 512].bitcast(I32)
                scl = stage[:, slot, WORDS + half * 512:WORDS + (half + 1) * 512]
                dve.wait_ge(raw_in[slot], 32 * (in_slot + 1))
                own.run(V.scalar_tensor_tensor(raw, raw, 12, raw, ALU.logical_shift_left, ALU.bitwise_or))
                own.run(V.tensor_scalar(mag[:, :], raw, 0x00070007, 9, ALU.bitwise_and,
                                        ALU.logical_shift_left))
                own.run(V.tensor_scalar(raw, raw, 0x00080008, 12, ALU.bitwise_and, ALU.logical_shift_left))
                own.run(V.tensor_tensor(raw, raw, mag[:, :], ALU.bitwise_or))
                val = stage[:, slot, half * 512:(half + 1) * 512].bitcast(F16)
                for i in range(2):
                    k = 4 * n + 2 * half + i
                    if not (isinstance(k, int) and k < 2):
                        dve.wait_ge(f_done, k - 1)
                    if m < 2:
                        v = val[:, 512 * i:512 * (i + 1)].rearrange("p (w k) -> p k w", k=2)
                        s = scl[:, 256 * i:256 * (i + 1)].unsqueeze(1).broadcast_to([P, 2, 256])
                        o = wf[:, i, :].rearrange("p (k w) -> p k w", k=2)
                    else:
                        v = val.rearrange("p (w k) -> p k w", k=2)[:, i, :]
                        s, o = scl, wf[:, i, :]
                    V.scalar_tensor_tensor(o, v, s_ffn[:, m:m + 1], s, ALU.mult, ALU.mult)\
                        .then_inc(wf_ready, 1)

            def group_0_piece(t, c):
                for m, half in group_0_pieces.get((t, c), ()):
                    dequantise(m, m % 2, 0, m, half, m // 2)

            def attention(t):
                first, last = t == 0, t == TILES - 1
                group_0_piece(t, 0)
                if not first:
                    x_lo(norm_2(t - 1), t - 1)
                unit(t, 0)
                if not last:
                    norm_1_of(t + 1)
                if first:
                    max_of(5)
                    scale(5)
                y_lo(t, 0)
                group_0_piece(t, 1)
                unit(t, 1)
                y_lo(t, 1)
                if not last:
                    x_lo(norm_1(t + 1), t + 1)
                group_0_piece(t, 2)
                unit(t, 2)
                y_lo(t, 2)
                unit(t, 3)
                y_lo(t, 3)
                group_0_piece(t, 3)
                if first:
                    max_of(6)
                    scale(6)
                own.restart()

            def add_attention(t, b):
                dve.wait_ge(attn_out, BLOCKS * t + b + 1)
                blk = h[:, t * BLOCKS + b, :]
                V.scalar_tensor_tensor(blk, ps[:, b, :], undo_out[:, 0:1], blk, ALU.mult, ALU.add)\
                    .then_inc(attn_added, 1)

            def attention_end(t):
                last = t == TILES - 1
                for b in range(BLOCKS):
                    if last and b == 2:
                        ffn_step(1, 1)
                    add_attention(t, b)
                    if b == 0 and not last:
                        rinv_of(t + 1)
                    if b > 0:
                        dve.wait_ge(attn_added, BLOCKS * t + b)
                        norm_stats(t, b - 1)
                    if b == 2 and not last:
                        split_rinv()
                dve.wait_ge(attn_added, BLOCKS * t + BLOCKS)
                norm_stats(t, BLOCKS - 1)
                if not last:
                    norm(norm_2(t), t)
                    norm_q(t + 1)

            def add_down(tile_index, t):
                for b in range(BLOCKS):
                    dve.wait_ge(down_made, BLOCKS * tile_index + b + 1)
                    blk = h[:, t * BLOCKS + b, :]
                    V.scalar_tensor_tensor(blk, ps[:, b, :], undo_down[:, 0:1], blk, ALU.mult, ALU.add)\
                        .then_inc(down_added, 1)

            def ffn_step(s, index, piece=None):
                b = s % 2
                gate, up = ps[:, 4 + 2 * b, :], ps[:, 5 + 2 * b, :]
                dve.wait_ge(gate_squared, index + 1)
                own.run(V.tensor_scalar(sq[:, b, :], sq[:, b, :], GELU_A, 1.0, ALU.mult, ALU.add))
                V.tensor_tensor(sq[:, b, :], sq[:, b, :], gate, ALU.mult).then_inc(inner_ready, 1)
                if piece:
                    dequantise(*piece)
                dve.wait_ge(tanh_done, index + 1)
                own.run(V.scalar_tensor_tensor(th[:, b, :], th[:, b, :], 1.0, gate, ALU.add, ALU.mult))
                dve.wait_ge(up_made, index + 1)
                V.scalar_tensor_tensor(th[:, b, :], th[:, b, :],
                                       0.5 * 2.0 ** (I_EXP - 2 * (F_EXP + X_EXP)), up,
                                       ALU.mult, ALU.mult).then_inc(inter_ready, 1)
                dve.wait_ge(inter_hi, index + 1)
                V.tensor_tensor(inter[:, b, 1, :], th[:, b, :], inter[:, b, 0, :], ALU.subtract)\
                    .then_inc(inter_done, 1)

            def ffn_group(group, par, pair, first=False, last=False):
                for s in range(2 if first else 0, STEPS):
                    piece = None
                    if s % 2 == 1 and 3 <= s < 15 and not last:
                        m, half = (s - 3) // 4, (s - 3) // 2 % 2
                        n = 6 * pair + 3 * (par + 1) + m
                        piece = (n, (par + 1 + m) % 2, 1 - par, m, half, 3 * pair + (3 * (par + 1) + m) // 2)
                    ffn_step(s, STEPS * group + s, piece)
                    if first and s == 2:
                        norm(norm_2(TILES - 1), TILES - 1, xn_last)
                    if s % GROUP == 0:
                        add_down(TILES * group + s // GROUP - 1, (s // GROUP - 1) % TILES)
                    if first and s == GROUP:
                        x_lo(norm_2(TILES - 1), TILES - 1, 0)
                own.restart()

            s_ffn = s_w[:, 6:9]
            V.memset(starts[:, :], 0.0).then_inc(zeros_ready, 1)
            dve.wait_ge(ids_in, 16)
            own.run(V.tensor_scalar(ids_f[:, 0, :], ids_sb[:, :], 0.0, float(VOCAB), ALU.is_lt, ALU.mult))
            own.run(V.tensor_tensor(ids_f[:, 1, :], ids_f[:, 0, :], ids_sb[:, :], ALU.add))
            V.tensor_scalar(rows[:, :], ids_f[:, 1, :], 0.0, float(VOCAB - 1), ALU.max, ALU.min)\
                .then_inc(rows_ready, 1)
            max_of(0)
            scale(0)
            max_of(1)
            scale(1)
            norm_1_of(0)
            split_lo(0)
            x_lo(0, 0, 0)
            split_lo(1)
            max_of(2)
            scale(2)
            max_of(3)
            scale(3)
            rinv_of(0)
            split_lo(2)
            split_rinv()
            split_lo(3)
            norm_q(0)
            max_of(4)
            scale(4)
            own.restart()
            for t in range(TILES):
                attention(t)
                if t == TILES - 1:
                    ffn_step(0, 0)
                attention_end(t)
            ffn_group(0, 0, 0, first=True)
            ffn_group(1, 1, 0)
            with dve.Fori(1, PAIRS - 1) as pair:
                ffn_group(2 * pair, 0, pair)
                ffn_group(2 * pair + 1, 1, pair)
            ffn_group(GROUPS - 2, 0, PAIRS - 1)
            ffn_group(GROUPS - 1, 1, PAIRS - 1, last=True)
            add_down(TILES * GROUPS - 1, TILES - 1)


def kernel(x, L0_tok_E, L0_tok_P, L0_attn_w_in, L0_attn_w_out, L0_ffn_gate_W_packed, L0_ffn_gate_scales,
           L0_ffn_up_W_packed, L0_ffn_up_scales, L0_ffn_down_W_packed, L0_ffn_down_scales):
    import numpy as np
    import concourse.bacc as bacc
    from concourse.bass_utils import run_bass_kernel_spmd

    def array(a):
        return np.asarray(a)

    def rows_by_channel(w):
        m = w.shape[0]
        return w.reshape(m, 2, P, 2).transpose(2, 3, 1, 0).reshape(P, KT, m)

    def up_words(w):
        return w.reshape(GROUPS, 2, P, 2, 2, P).transpose(0, 5, 1, 3, 4, 2).reshape(GROUPS, P, WORDS)

    def up_scales(w):
        return w.reshape(GROUPS, 2, P, 2, 2, 8).transpose(0, 5, 1, 3, 4, 2).reshape(GROUPS, 8, WORDS)

    def down_words(w):
        return w.reshape(D, GROUPS, 2, P).transpose(1, 3, 2, 0).reshape(GROUPS, P, WORDS)

    def down_scales(w):
        return w.reshape(D, GROUPS, 2, 8).transpose(1, 3, 2, 0).reshape(GROUPS, 8, WORDS)

    gate_s, up_s, down_s = (array(a) for a in (L0_ffn_gate_scales, L0_ffn_up_scales, L0_ffn_down_scales))
    w_in = rows_by_channel(array(L0_attn_w_in))
    arrays = {
        "ids": array(x).T,
        "table": array(L0_tok_E),
        "p_t": array(L0_tok_P).T,
        "w_in": np.concatenate([w_in[None, :, :, 0:D], w_in[:, :, D:].reshape(P, KT, 4, CT, P)
                                .transpose(3, 0, 1, 2, 4).reshape(CT, P, KT, D)]).reshape(1 + CT, P, KT * D),
        "w_out": array(L0_attn_w_out).T.reshape(CT, P, D).transpose(1, 0, 2).reshape(P, CT * D),
        "all_scales": np.concatenate([a.reshape(P, 512) for a in (gate_s, up_s, down_s)], axis=1),
        "packed": np.stack([up_words(array(L0_ffn_gate_W_packed)), up_words(array(L0_ffn_up_W_packed)),
                            down_words(array(L0_ffn_down_W_packed))], axis=1).reshape(3 * GROUPS, P, WORDS),
        "scales": np.stack([up_scales(gate_s), up_scales(up_s), down_scales(down_s)],
                           axis=1).reshape(3 * GROUPS, 8, WORDS),
    }
    arrays = {k: np.ascontiguousarray(v) for k, v in arrays.items()}
    nc = bacc.Bacc("TRN2", target_bir_lowering=False, num_devices=1)
    aps = [nc.dram_tensor(k, v.shape, mybir.dt.from_np(v.dtype), kind="ExternalInput").ap()
           for k, v in arrays.items()]
    out = nc.dram_tensor("out", (SEQS, SEQ_LEN, D), F32, kind="ExternalOutput").ap()
    lm_layer(nc, *aps, out.rearrange("s p d -> p s d"))
    result = run_bass_kernel_spmd(nc, [arrays], core_ids=[0])
    return result.results[0]["out"]
```
